# Optimizing a Trainium2 kernel written in Bass

```python
import numpy as np
import jax
import jax.numpy as jnp

def _softmax(x, axis=-1):
    return jax.nn.softmax(x, axis=axis)

def _gelu(x):
    return jax.nn.gelu(x, approximate=True)

def _silu(x):
    return jax.nn.silu(x)

def _sigmoid(x):
    return jax.nn.sigmoid(x)

def _layernorm(x, axis=-1, eps=1e-05):
    m = jnp.mean(x, axis=axis, keepdims=True)
    v = jnp.var(x, axis=axis, keepdims=True)
    return (x - m) / jnp.sqrt(v + eps)

def _scatter_add(tgt, idx, src, axis=0):
    return tgt.at[idx].add(src)

def _segment_sum(src, seg, n):
    return jax.ops.segment_sum(src, seg, n)
kernel_name = 'mk_xattn_ffn_d2_seqx_r4_e6f02d'

def setup_inputs(seed: int=0):
    np.random.seed(seed)
    _w = jnp.asarray

    def _rec_inputs():
        import jax
        import jax.numpy as jnp
        _rk = jax.random.key(seed)
        x = 7.22e-05 + 1 * jax.random.normal(jax.random.fold_in(_rk, 1), (64, 128, 512), jnp.float32)
        _lenS = 128 - jax.random.randint(jax.random.fold_in(_rk, 7), (64,), 0, max(1, 128 // 4) + 1, jnp.int32)
        _lenS2 = 128 - jax.random.randint(jax.random.fold_in(_rk, 8), (64,), 0, max(1, 128 // 4) + 1, jnp.int32)
        _ctx_2048P = jax.random.normal(jax.random.fold_in(_rk, 11), (64, 16, 512), jnp.float32)
        _ctx_2048c = jax.random.dirichlet(jax.random.fold_in(_rk, 511), 0.3 * jnp.ones((16,), jnp.float32), (64, 128))
        _ctx_2048t = jnp.einsum('bsk,bkd->bsd', _ctx_2048c, _ctx_2048P)
        _ctx_2048t = _ctx_2048t * jax.lax.rsqrt(jnp.mean(jnp.square(_ctx_2048t)) + 1e-12) * 0.953939
        ctx_2048 = 4.13588e-05 + 0.999923 * (_ctx_2048t + 0.3 * jax.random.normal(jax.random.fold_in(_rk, 611), (64, 128, 512), jnp.float32))
        return (x, ctx_2048)
    x, ctx_2048 = _rec_inputs()

    def _L0_xattn_setup():
        import jax, jax.numpy as jnp
        import numpy as np
        N_HEAD = 8
        key = jax.random.key(seed)
        k1, k2, k3 = jax.random.split(key, 3)
        b, d, m = (4, 256, 512)
        c, n = (256, 512)
        q = jax.random.normal(k1, (b, d, m), dtype=jnp.float32)
        k = jax.random.normal(k2, (d // d * b, d, n), dtype=jnp.float32).reshape(b, d, n)
        v = jax.random.normal(k3, (b, c, n), dtype=jnp.float32)
        return {'q': q, 'k': k, 'v': v}
    _L0_xattn_all = _L0_xattn_setup()
    _L0_xattn_in = {k: v for k, v in _L0_xattn_all.items() if k in ()}
    del _L0_xattn_all

    def _L0_ffn_setup():
        import jax, jax.numpy as jnp
        import numpy as np

        def fwht(x):
            n = x.shape[-1]
            orig_shape = x.shape
            x = x.reshape(-1, n)
            h = 1
            while h < n:
                x = x.reshape(-1, n // (2 * h), 2, h)
                a = x[:, :, 0, :]
                b = x[:, :, 1, :]
                x = jnp.stack([a + b, a - b], axis=2)
                h *= 2
            x = x.reshape(orig_shape)
            return x * (1.0 / jnp.sqrt(jnp.asarray(n, dtype=x.dtype)))

        def act_quant(x, bits):
            qb = 2.0 ** (bits - 1) - 1.0
            scale = qb / jnp.clip(jnp.max(jnp.abs(x), axis=-1, keepdims=True), 1e-05, None)
            q = jnp.clip(jnp.round(x * scale), -qb, qb) / scale
            return x + jax.lax.stop_gradient(q - x)

        def weight_quant(w):
            scale = jnp.clip(jnp.mean(jnp.abs(w)), 1e-05, None)
            q = jnp.clip(jnp.round(w / scale), -1.0, 1.0) * scale
            return w + jax.lax.stop_gradient(q - w)

        def hbitlinear(x, w, bits):
            xh = fwht(x)
            xq = act_quant(xh, bits)
            wq = weight_quant(w)
            return jnp.einsum('bsh,oh->bso', xq, wq)
        key = jax.random.key(seed)
        k1, k2, k3 = jax.random.split(key, 3)
        B, S, H = (4, 512, 512)
        I = 1024
        hidden_states = jax.random.normal(k1, (B, S, H), dtype=jnp.float32)
        w_up = jax.random.normal(k2, (I, H), dtype=jnp.float32) * 0.02
        w_down = jax.random.normal(k3, (H, I), dtype=jnp.float32) * 0.02
        return {'hidden_states': hidden_states, 'w_up': w_up, 'w_down': w_down}
    _L0_ffn_all = _L0_ffn_setup()
    _L0_ffn_in = {k: v for k, v in _L0_ffn_all.items() if k in ('w_up', 'w_down')}
    del _L0_ffn_all

    def _L1_xattn_setup():
        import math
        import jax, jax.numpy as jnp
        import numpy as np
        HEADS = 16
        MASKED_BIAS = -10000.0

        def _mha(q, k, v):
            B, Sq, D = q.shape
            Sk = k.shape[-2]
            hd = D // HEADS
            qh = q.reshape(B, Sq, HEADS, hd).transpose(0, 2, 1, 3)
            kh = k.reshape(B, Sk, HEADS, hd).transpose(0, 2, 1, 3)
            vh = v.reshape(B, Sk, HEADS, hd).transpose(0, 2, 1, 3)
            scores = jnp.einsum('bhqd,bhkd->bhqk', qh, kh) / math.sqrt(hd)
            qi = jnp.arange(Sq)[:, None] + (Sk - Sq)
            ki = jnp.arange(Sk)[None, :]
            causal = ki <= qi
            scores = jnp.where(causal[None, None], scores, jnp.asarray(MASKED_BIAS, scores.dtype))
            attn = jax.nn.softmax(scores, axis=-1)
            out = jnp.einsum('bhqk,bhkd->bhqd', attn, vh)
            return out.transpose(0, 2, 1, 3).reshape(B, Sq, D)
        key = jax.random.key(seed)
        kq, kk, kv = jax.random.split(key, 3)
        B, S, D = (4, 256, 512)
        q = jax.random.normal(kq, (B, S, D), dtype=jnp.float32)
        k = jax.random.normal(kk, (B, S, D), dtype=jnp.float32)
        v = jax.random.normal(kv, (B, S, D), dtype=jnp.float32)
        return {'q': q, 'k': k, 'v': v}
    _L1_xattn_all = _L1_xattn_setup()
    _L1_xattn_in = {k: v for k, v in _L1_xattn_all.items() if k in ()}
    del _L1_xattn_all

    def _L1_ffn_setup():
        import jax, jax.numpy as jnp
        import numpy as np
        B, L, D = (4, 512, 512)
        S, K, NB = (16, 4, 2)
        H = D // 64
        EPS = 1e-06

        def _rms(x, w):
            return x * jax.lax.rsqrt(jnp.mean(x * x, axis=-1, keepdims=True) + EPS) * w
        key = jax.random.key(seed)
        ks = jax.random.split(key, 8)
        g = lambda k, shape, s: jax.random.normal(k, shape, dtype=jnp.float32) * s
        return {'x': g(ks[0], (B, L, D), 1.0), 'workspace': g(ks[1], (S, D), 0.02), 'compete_w': g(ks[2], (S, D), 0.02), 'compete_b': jnp.zeros((S,), jnp.float32), 'write_w': g(ks[3], (D, D), 0.02), 'write_b': jnp.zeros((D,), jnp.float32), 'in_proj_w': g(ks[4], (3 * D, D), 0.02), 'in_proj_b': jnp.zeros((3 * D,), jnp.float32), 'out_proj_w': g(ks[5], (D, D), 0.02), 'out_proj_b': jnp.zeros((D,), jnp.float32), 'ig_w': g(ks[6], (1, D), 0.02), 'ig_b': jnp.zeros((1,), jnp.float32), 'norm_pre_w': jnp.ones((D,), jnp.float32), 'norm_post_w': jnp.ones((D,), jnp.float32)}
    _L1_ffn_all = _L1_ffn_setup()
    _L1_ffn_in = {k: v for k, v in _L1_ffn_all.items() if k in ('workspace', 'compete_w', 'compete_b', 'write_w', 'write_b', 'in_proj_w', 'in_proj_b', 'out_proj_w', 'out_proj_b', 'ig_w', 'ig_b', 'norm_pre_w', 'norm_post_w')}
    del _L1_ffn_all
    return {'x': x, 'ctx_2048': ctx_2048, 'L0_ffn_w_up': _L0_ffn_in['w_up'], 'L0_ffn_w_down': _L0_ffn_in['w_down'], 'L1_ffn_workspace': _L1_ffn_in['workspace'], 'L1_ffn_compete_w': _L1_ffn_in['compete_w'], 'L1_ffn_compete_b': _L1_ffn_in['compete_b'], 'L1_ffn_write_w': _L1_ffn_in['write_w'], 'L1_ffn_write_b': _L1_ffn_in['write_b'], 'L1_ffn_in_proj_w': _L1_ffn_in['in_proj_w'], 'L1_ffn_in_proj_b': _L1_ffn_in['in_proj_b'], 'L1_ffn_out_proj_w': _L1_ffn_in['out_proj_w'], 'L1_ffn_out_proj_b': _L1_ffn_in['out_proj_b'], 'L1_ffn_ig_w': _L1_ffn_in['ig_w'], 'L1_ffn_ig_b': _L1_ffn_in['ig_b'], 'L1_ffn_norm_pre_w': _L1_ffn_in['norm_pre_w'], 'L1_ffn_norm_post_w': _L1_ffn_in['norm_post_w']}

def reference(x, ctx_2048, L0_ffn_w_up, L0_ffn_w_down, L1_ffn_workspace, L1_ffn_compete_w, L1_ffn_compete_b, L1_ffn_write_w, L1_ffn_write_b, L1_ffn_in_proj_w, L1_ffn_in_proj_b, L1_ffn_out_proj_w, L1_ffn_out_proj_b, L1_ffn_ig_w, L1_ffn_ig_b, L1_ffn_norm_pre_w, L1_ffn_norm_post_w):
    import jax
    import jax.numpy as jnp

    def _L0_xattn_ref(q, k, v):
        import jax, jax.numpy as jnp
        import numpy as np
        N_HEAD = 8
        b, d, m = q.shape
        c = v.shape[1]
        h = N_HEAD
        qh = q.reshape(b * h, d // h, m)
        kh = k.reshape(b * h, d // h, -1)
        vh = v.reshape(b * h, c // h, -1)
        scale = 1.0 / jnp.sqrt(jnp.asarray(d // h, dtype=q.dtype))
        qk = jnp.einsum('bdm,bdn->bmn', qh, kh) * scale
        sm = jax.nn.softmax(qk, axis=-1)
        ret = jnp.einsum('bmn,bcn->bcm', sm, vh)
        return ret.reshape(b, c, m)

    def _L0_ffn_ref(hidden_states, w_up, w_down):
        import jax, jax.numpy as jnp
        import numpy as np

        def fwht(x):
            n = x.shape[-1]
            orig_shape = x.shape
            x = x.reshape(-1, n)
            h = 1
            while h < n:
                x = x.reshape(-1, n // (2 * h), 2, h)
                a = x[:, :, 0, :]
                b = x[:, :, 1, :]
                x = jnp.stack([a + b, a - b], axis=2)
                h *= 2
            x = x.reshape(orig_shape)
            return x * (1.0 / jnp.sqrt(jnp.asarray(n, dtype=x.dtype)))

        def act_quant(x, bits):
            qb = 2.0 ** (bits - 1) - 1.0
            scale = qb / jnp.clip(jnp.max(jnp.abs(x), axis=-1, keepdims=True), 1e-05, None)
            q = jnp.clip(jnp.round(x * scale), -qb, qb) / scale
            return x + jax.lax.stop_gradient(q - x)

        def weight_quant(w):
            scale = jnp.clip(jnp.mean(jnp.abs(w)), 1e-05, None)
            q = jnp.clip(jnp.round(w / scale), -1.0, 1.0) * scale
            return w + jax.lax.stop_gradient(q - w)

        def hbitlinear(x, w, bits):
            xh = fwht(x)
            xq = act_quant(xh, bits)
            wq = weight_quant(w)
            return jnp.einsum('bsh,oh->bso', xq, wq)
        ACT_BITS = 8
        h = hbitlinear(hidden_states, w_up, ACT_BITS)
        h = jnp.square(jax.nn.relu(h))
        out = hbitlinear(h, w_down, ACT_BITS)
        return out

    def _L1_xattn_ref(q, k, v):
        import math
        import jax, jax.numpy as jnp
        import numpy as np
        HEADS = 16
        MASKED_BIAS = -10000.0

        def _mha(q, k, v):
            B, Sq, D = q.shape
            Sk = k.shape[-2]
            hd = D // HEADS
            qh = q.reshape(B, Sq, HEADS, hd).transpose(0, 2, 1, 3)
            kh = k.reshape(B, Sk, HEADS, hd).transpose(0, 2, 1, 3)
            vh = v.reshape(B, Sk, HEADS, hd).transpose(0, 2, 1, 3)
            scores = jnp.einsum('bhqd,bhkd->bhqk', qh, kh) / math.sqrt(hd)
            qi = jnp.arange(Sq)[:, None] + (Sk - Sq)
            ki = jnp.arange(Sk)[None, :]
            causal = ki <= qi
            scores = jnp.where(causal[None, None], scores, jnp.asarray(MASKED_BIAS, scores.dtype))
            attn = jax.nn.softmax(scores, axis=-1)
            out = jnp.einsum('bhqk,bhkd->bhqd', attn, vh)
            return out.transpose(0, 2, 1, 3).reshape(B, Sq, D)
        return _mha(q, k, v)

    def _L1_ffn_ref(x, workspace, compete_w, compete_b, write_w, write_b, in_proj_w, in_proj_b, out_proj_w, out_proj_b, ig_w, ig_b, norm_pre_w, norm_post_w):
        import jax, jax.numpy as jnp
        import numpy as np
        B, L, D = (4, 512, 512)
        S, K, NB = (16, 4, 2)
        H = D // 64
        EPS = 1e-06

        def _rms(x, w):
            return x * jax.lax.rsqrt(jnp.mean(x * x, axis=-1, keepdims=True) + EPS) * w
        Bq, Lq, Dd = x.shape
        hd = Dd // H
        scale = 1.0 / np.sqrt(hd).astype(np.float32)
        ws = jnp.broadcast_to(workspace[None], (Bq, S, Dd))
        wq, wk, wv = (in_proj_w[:Dd], in_proj_w[Dd:2 * Dd], in_proj_w[2 * Dd:])
        bq, bk, bv = (in_proj_b[:Dd], in_proj_b[Dd:2 * Dd], in_proj_b[2 * Dd:])
        k_eff = min(K, Lq)
        for _ in range(NB):
            logits = _rms(x, norm_pre_w) @ compete_w.T + compete_b
            slot_logits = jnp.swapaxes(logits, 1, 2)
            vals, idx = jax.lax.top_k(slot_logits, k_eff)
            wgt = jax.nn.softmax(vals, axis=-1)
            wx = x @ write_w.T + write_b
            gathered = jnp.take_along_axis(wx[:, None], idx[..., None], axis=2)
            written = jnp.einsum('bsk,bskd->bsd', wgt, gathered)
            ws = _rms(ws + written, norm_post_w)
            q = (x @ wq.T + bq).reshape(Bq, Lq, H, hd)
            kk = (ws @ wk.T + bk).reshape(Bq, S, H, hd)
            vv = (ws @ wv.T + bv).reshape(Bq, S, H, hd)
            att = jax.nn.softmax(jnp.einsum('blhd,bshd->bhls', q, kk) * scale, axis=-1)
            ctx = jnp.einsum('bhls,bshd->blhd', att, vv).reshape(Bq, Lq, Dd)
            x_b = ctx @ out_proj_w.T + out_proj_b
            x = _rms(x + x_b, norm_post_w)
            ignition = jax.nn.sigmoid(x @ ig_w.T + ig_b)
        return x
    x = x + _L0_xattn_ref(_layernorm(x, axis=-1), ctx_2048, ctx_2048)
    x = x + _L0_ffn_ref(_layernorm(x, axis=-1), L0_ffn_w_up, L0_ffn_w_down)
    x = x + _L1_xattn_ref(_layernorm(x, axis=-1), ctx_2048, ctx_2048)
    x = x + _L1_ffn_ref(_layernorm(x, axis=-1), L1_ffn_workspace, L1_ffn_compete_w, L1_ffn_compete_b, L1_ffn_write_w, L1_ffn_write_b, L1_ffn_in_proj_w, L1_ffn_in_proj_b, L1_ffn_out_proj_w, L1_ffn_out_proj_b, L1_ffn_ig_w, L1_ffn_ig_b, L1_ffn_norm_pre_w, L1_ffn_norm_post_w)
    return x

_drawn_inputs = setup_inputs


def setup_inputs(seed=0):
    import zlib

    import numpy as np

    out = dict(_drawn_inputs(seed))
    spreads = {'L1_ffn_compete_b': (0.0, 2.0),
     'L1_ffn_write_b': (0.0, 0.1),
     'L1_ffn_in_proj_b': (0.0, 0.1),
     'L1_ffn_out_proj_b': (0.0, 0.1),
     'L1_ffn_norm_pre_w': (1.0, 0.6),
     'L1_ffn_norm_post_w': (1.0, 0.2)}
    factors = {'L1_ffn_workspace': 21.942, 'L1_ffn_compete_w': 2.805}
    for name, (base, spread) in spreads.items():
        noise = np.random.default_rng([zlib.crc32(name.encode()), seed]).standard_normal(out[name].shape)
        drawn = base * np.exp(spread * noise) if base else spread * noise
        out[name] = jnp.asarray(drawn.astype(out[name].dtype))
    for name, factor in factors.items():
        out[name] = (out[name] * factor).astype(out[name].dtype)
    return out
```

```python
from contextlib import ExitStack

import concourse.bass as bass
from concourse import mybir

F32 = mybir.dt.float32
BF16 = mybir.dt.bfloat16
ALU = mybir.AluOpType
ACT = mybir.ActivationFunctionType
AX = mybir.AxisListType


def at_least(eng, sem, count):
    if isinstance(count, int) and count <= 0:
        return
    assert isinstance(count, int) or count.min_val >= 1
    eng.wait_ge(sem, count)


class Held:

    def __init__(self, eng, passed):
        self.eng, self.passed = eng, passed

    def wait_ge(self, sem, count):
        self.eng.wait_ge(sem, count)
        if not isinstance(count, int):
            self.eng.sem_inc(self.passed, 1)


class Semaphores:

    def __init__(self, nc, prefix, stack):
        self.nc, self.prefix, self.handles = nc, prefix, []
        stack.callback(self.clear)

    def __call__(self, name):
        self.handles.append(self.nc.alloc_semaphore(self.prefix + name))
        return self.handles[-1]

    def clear(self):
        self.nc.clear_and_free_semaphores(self.handles)
        self.nc.all_engine_barrier()


class Step:

    GROUPS, SLOTS = 128, 3

    def __init__(self, turn, k):
        self.turn, self.k = turn, k

    def exists(self, ahead):
        return not isinstance(self.turn, int) or 0 <= self.k + ahead < self.GROUPS

    def group(self, ahead):
        return self.turn * 6 + (self.k + ahead)

    def batch(self, ahead):
        return self.turn * 3 + (self.k + ahead) // 2

    def half(self, ahead):
        return (self.k + ahead) % 2

    def slot(self, ahead):
        return (self.k + ahead) // 2 % self.SLOTS

    def lap(self, ahead):
        return self.turn + (self.k + ahead) // 6

    def pair(self, ahead):
        return self.turn * 3 + (self.k + ahead) // 2


def run_steps(eng, first, loop_from, loop_to, last, body):
    assert (loop_to - loop_from) % 6 == 0
    for k in range(first, loop_from):
        body(Step(0, k))
    with eng.Fori(0, (loop_to - loop_from) // 6) as turn:
        for k in range(6):
            body(Step(turn, loop_from + k))
    for k in range(loop_to, last + 1):
        body(Step(0, k))


def attention0(nc, x, ctx, ctxT, ident, q_parts, k_parts, heads_out):
    B, C, M = x.shape
    D = 16
    H = C // D
    G = 4
    GROUPS = B * H // G
    NT = M // 128
    KROW = 6 * D
    KALL = KROW + 2
    EPS = 1e-5
    NB = Step.SLOTS
    SCALE = float(D) ** -0.5
    assert GROUPS == Step.GROUPS

    with ExitStack() as st:
        def sb(name, shape, dt):
            return st.enter_context(nc.sbuf_tensor("a_" + name, shape, dt))

        def ps(name, shape, dt):
            return st.enter_context(nc.psum_tensor("a_" + name, shape, dt))

        sem = Semaphores(nc, "a_", st)

        x_in = sb("x_in", [128, NB, M], F32)
        c_in = sb("c_in", [128, NB, M], F32)
        cT_in = sb("cT_in", [128, NB, NT, C], F32)
        z = sb("z", [128, M], F32)
        rest = sb("rest", [128, 2, M], F32)
        q_split = sb("q_split", [128, NB, 3, M], BF16)
        k_split = sb("k_split", [128, NB, 3, M], BF16)
        stats = sb("stats", [128, 6], F32)
        mean_var = sb("mean_var", [128, NB, 2], F32)
        var_eps = sb("var_eps", [128, 1], F32)
        rstd = sb("rstd", [128, 1], F32)
        neg_half = sb("neg_half", [128, 1], F32)
        Q = [sb(f"Q{i}", [KALL, H, M], BF16) for i in range(NB)]
        K = [sb(f"K{i}", [KALL, H, M], BF16) for i in range(NB)]
        V = [sb(f"V{i}", [128, NT, H, 32], F32) for i in range(NB)]
        P = [[sb(f"P{i}_{j}", [128, NT, M], F32) for j in range(G)] for i in range(2)]
        neg_max = sb("neg_max", [128, 2, G * NT], F32)
        max_parts = sb("max_parts", [128, 2, 2 * G * NT], BF16)
        max_rows = sb("max_rows", [2 * G * NT, 2, 128], BF16)
        out_sb = sb("out_sb", [128, 2, M], F32)
        identf = sb("identf", [128, 128], F32)
        identb = sb("identb", [128, 128], BF16)

        max_ps = [ps(f"max_ps{i}", [128, 2, M], F32) for i in range(2)]
        sc_ps = [ps(f"sc_ps{i}", [128, M], F32) for i in range(2)]
        pv_ps = ps("pv_ps", [128, M], F32)
        turn_ps = ps("turn_ps", [2 * G * NT, 128], BF16)

        ident_loaded, ident_ready, preset = sem("ident_loaded"), sem("ident_ready"), sem("preset")
        x_loaded = [sem(f"x_loaded{i}") for i in range(NB)]
        c_loaded = [sem(f"c_loaded{i}") for i in range(NB)]
        cT_loaded = [sem(f"cT_loaded{i}") for i in range(NB)]
        Q_loaded = [sem(f"Q_loaded{i}") for i in range(NB)]
        K_loaded = [sem(f"K_loaded{i}") for i in range(NB)]
        q_stored = [sem(f"q_stored{i}") for i in range(NB)]
        k_stored = [sem(f"k_stored{i}") for i in range(NB)]
        max_rows_in_Q = [sem(f"max_rows_in_Q{i}") for i in range(2)]
        out_stored = [sem(f"out_stored{i}") for i in range(2)]
        stats_done, moments_done, pool_chain = sem("stats_done"), sem("moments_done"), sem("pool_chain")
        q_split_done, k_split_done, v_done = sem("q_split_done"), sem("k_split_done"), sem("v_done")
        max_filled, max_taken = sem("max_filled"), sem("max_taken")
        max_hi_done, max_parts_done = sem("max_hi_done"), sem("max_parts_done")
        max_turned, max_rows_done = sem("max_turned"), sem("max_rows_done")
        scores_filled, exp_done = sem("scores_filled"), sem("exp_done")
        pv_done, out_copied = sem("pv_done"), sem("out_copied")
        sp_passed, pool_passed, dve_passed = sem("sp_passed"), sem("pool_passed"), sem("dve_passed")

        block = st.enter_context(nc.Block())

        def part_rows(parts, b, first, count, stride):
            v = parts[b].rearrange("t (h d) m -> t d h m", d=D)
            return v[first:first + stride * (count - 1) + 1:stride] if count > 1 else v[first:first + 1]

        @block.sync
        def _(sp):
            sp.dma_start(identf[:, :], ident).then_inc(ident_loaded, 16)
            sp.wait_ge(ident_loaded, 16)

            held = Held(sp, sp_passed)

            def step(s):
                if s.half(8) == 0 and s.exists(8):
                    b, i = s.batch(8), s.slot(8)
                    at_least(held, q_split_done, b - (NB - 1))
                    at_least(held, k_split_done, b - (NB - 1))
                    at_least(held, v_done, b - (NB - 1))
                    sp.dma_start(x_in[:, i, :], x[b]).then_inc(x_loaded[i], 16)
                    sp.dma_start(c_in[:, i, :], ctx[b]).then_inc(c_loaded[i], 16)
                    sp.dma_start(cT_in[:, i, :, :], ctxT[b].rearrange("(t p) c -> p t c", p=128)).then_inc(cT_loaded[i], 16)
                if s.half(5) == 0 and s.exists(5):
                    b, i = s.batch(5), s.slot(5)
                    held.wait_ge(q_split_done, b + 1)
                    sp.dma_start(q_parts[b].rearrange("t c m -> c t m"), q_split[:, i, :, :]).then_inc(q_stored[i], 16)
                    held.wait_ge(k_split_done, b + 1)
                    sp.dma_start(k_parts[b].rearrange("t c m -> c t m"), k_split[:, i, :, :]).then_inc(k_stored[i], 16)
                if s.half(4) == 0 and s.exists(4):
                    b, i = s.batch(4), s.slot(4)
                    held.wait_ge(q_stored[i], s.lap(4) * 16 + 16)
                    held.wait_ge(k_stored[i], s.lap(4) * 16 + 16)
                    at_least(held, scores_filled, (b - (NB - 1)) * (2 * G * NT))
                    row = 0
                    for first, count, stride in ((0, 1, 1), (0, 1, 1), (1, 1, 1), (1, 1, 1), (0, 1, 1), (2, 1, 1)):
                        sp.dma_start(Q[i][row:row + D, :, :], part_rows(q_parts, b, first, 1, 1)[0]).then_inc(Q_loaded[i], 16)
                        row += D
                    row = 0
                    for first in (0, 1, 0, 1, 2, 0):
                        sp.dma_start(K[i][row:row + D, :, :], part_rows(k_parts, b, first, 1, 1)[0]).then_inc(K_loaded[i], 16)
                        row += D
            run_steps(sp, -8, 2, 116, 126, step)
            for i in range(2):
                sp.wait_ge(out_stored[i], 16 * GROUPS // 2)

        @block.gpsimd
        def _(pool):
            pool.memset(neg_half[:, :], -0.5).then_inc(preset, 1)
            pool.wait_ge(preset, 1)
            for i in range(NB):
                pool.memset(K[i][KROW:KALL, :, :], 1.0).then_inc(preset, 1)
                pool.wait_ge(preset, 2 + 2 * i)
                pool.memset(V[i][:, :, :, D:2 * D], 1.0).then_inc(preset, 1)
                pool.wait_ge(preset, 3 + 2 * i)
            held = Held(pool, pool_passed)
            LINKS = 9

            def step(s):
                if s.half(6) == 0 and s.exists(6):
                    b, i = s.batch(6), s.slot(6)

                    def link(n, ins):
                        ins.then_inc(pool_chain, 1)
                        held.wait_ge(pool_chain, b * LINKS + n)
                    held.wait_ge(moments_done, b + 1)
                    link(1, pool.tensor_scalar(var_eps[:, :], mean_var[:, i, 1:2], 1.0, EPS, ALU.mult, ALU.add))
                    link(2, pool.tensor_tensor(rstd[:, :], var_eps[:, :], neg_half[:, :], ALU.pow))
                    link(3, pool.tensor_scalar(z[:, :], x_in[:, i, :], mean_var[:, i, 0:1], rstd[:, :], ALU.subtract, ALU.mult))
                    at_least(held, q_stored[i], s.lap(6) * 16)
                    q = q_split[:, i]
                    link(4, pool.tensor_scalar(q[:, 0, :], z[:, :], 1.0, 0.0, ALU.mult, ALU.add))
                    link(5, pool.tensor_tensor(rest[:, 0, :], z[:, :], q[:, 0, :], ALU.subtract))
                    link(6, pool.tensor_scalar(q[:, 1, :], rest[:, 0, :], 1.0, 0.0, ALU.mult, ALU.add))
                    pool.tensor_tensor(q[:, 2, :], rest[:, 0, :], q[:, 1, :], ALU.subtract).then_inc(q_split_done, 1)
                    held.wait_ge(q_split_done, b + 1)
                if s.half(5) == 0 and s.exists(5):
                    b, i = s.batch(5), s.slot(5)

                    def link(n, ins):
                        ins.then_inc(pool_chain, 1)
                        held.wait_ge(pool_chain, b * LINKS + n)
                    held.wait_ge(c_loaded[i], s.lap(5) * 16 + 16)
                    at_least(held, k_stored[i], s.lap(5) * 16)
                    k = k_split[:, i]
                    link(7, pool.tensor_scalar(k[:, 0, :], c_in[:, i, :], 1.0, 0.0, ALU.mult, ALU.add))
                    link(8, pool.tensor_tensor(rest[:, 1, :], c_in[:, i, :], k[:, 0, :], ALU.subtract))
                    link(9, pool.tensor_scalar(k[:, 1, :], rest[:, 1, :], 1.0, 0.0, ALU.mult, ALU.add))
                    pool.tensor_tensor(k[:, 2, :], rest[:, 1, :], k[:, 1, :], ALU.subtract).then_inc(k_split_done, 1)
                    held.wait_ge(k_split_done, b + 1)
                if s.half(3) == 0 and s.exists(3):
                    b, i = s.batch(3), s.slot(3)
                    held.wait_ge(cT_loaded[i], s.lap(3) * 16 + 16)
                    at_least(held, pv_done, (b - (NB - 1)) * 2)
                    pool.tensor_scalar(V[i][:, :, :, 0:D], cT_in[:, i].rearrange("p t (h d) -> p t h d", d=D), 1.0, 0.0,
                                       ALU.mult, ALU.add).then_inc(v_done, 1)
            run_steps(pool, -6, 4, 118, 126, step)

        @block.vector
        def _(dve):
            dve.wait_ge(ident_loaded, 16)
            dve.tensor_copy(identb[:, :], identf[:, :]).then_inc(ident_ready, 1)
            held = Held(dve, dve_passed)

            def step(s):
                if s.exists(2):
                    g, p = s.group(2), s.half(2)
                    for u in range(2 * G):
                        dve.wait_ge(max_filled, g * (2 * G) + (u + 1))
                        dve.tensor_reduce(neg_max[:, p, 2 * u:2 * u + 2], max_ps[u % 2][:, :, :], AX.X, ALU.max,
                                          negate=True).then_inc(max_taken, 1)
                    dve.wait_ge(max_taken, g * (2 * G) + 2 * G)
                    at_least(dve, max_turned, g - 1)
                    dve.tensor_copy(max_parts[:, p, 0:G * NT], neg_max[:, p, :]).then_inc(max_hi_done, 1)
                    dve.wait_ge(max_hi_done, g + 1)
                    dve.tensor_tensor(max_parts[:, p, G * NT:2 * G * NT], neg_max[:, p, :], max_parts[:, p, 0:G * NT],
                                      ALU.subtract).then_inc(max_parts_done, 1)
                    dve.wait_ge(max_parts_done, g + 1)
                if s.half(7) == 0 and s.exists(7):
                    b, i = s.batch(7), s.slot(7)
                    dve.wait_ge(x_loaded[i], s.lap(7) * 16 + 16)
                    dve.bn_stats(stats[:, :], x_in[:, i, :]).then_inc(stats_done, 1)
                    at_least(dve, q_split_done, b - (NB - 1))
                    held.wait_ge(stats_done, b + 1)
                    dve.bn_aggr(mean_var[:, i, :], stats[:, :]).then_inc(moments_done, 1)
                    dve.wait_ge(moments_done, b + 1)
            run_steps(dve, -7, 1, 115, 125, step)

        @block.tensor
        def _(pe):
            pe.wait_ge(ident_ready, 1)
            pe.wait_ge(preset, 1 + 2 * NB)

            def step(s):
                for k in range(G * NT + 2):
                    if s.exists(2) and k % 2 == 0 and k < G * NT:
                        g, i, u = s.group(2), s.slot(2), k // 2
                        if u == 0 and s.half(2) == 0:
                            pe.wait_ge(Q_loaded[i], s.lap(2) * 96 + 96)
                            pe.wait_ge(K_loaded[i], s.lap(2) * 96 + 96)
                        at_least(pe, max_taken, g * (2 * G) + (u - 1))
                        h = s.half(2) * G + u // 2
                        for j in range(2):
                            m = (u % 2 * 2 + j) * 128
                            last = pe.matmul(max_ps[u % 2][:, j, :], Q[i][0:KROW, h, m:m + 128], K[i][0:KROW, h, :],
                                             start=True, stop=True)
                        last.then_inc(max_filled, 1)
                    if s.exists(1) and k == 1:
                        g, p = s.group(1), s.half(1)
                        pe.wait_ge(max_parts_done, g + 1)
                        at_least(pe, max_rows_done, g)
                        pe.transpose(turn_ps[:, :], max_parts[:, p, :], identb[:, :]).then_inc(max_turned, 1)
                    if s.exists(0) and k < G * NT:
                        g, i = s.group(0), s.slot(0)
                        if k == 0:
                            pe.wait_ge(max_rows_in_Q[s.half(0)], s.pair(0) * 32 + 32)
                        at_least(pe, exp_done, g * (G * NT) + (k - 1))
                        h, n = s.half(0) * G + k // NT, k % NT * 128
                        pe.matmul(sc_ps[k % 2][:, :], K[i][:, h, n:n + 128], Q[i][:, h, :],
                                  start=True, stop=True).then_inc(scores_filled, 1)
                    if s.exists(-1) and k >= 2:
                        g, i, p = s.group(-1), s.slot(-1), s.half(-1)
                        t, j = (k - 2) // G, (k - 2) % G
                        if k == 2:
                            pe.wait_ge(exp_done, g * (G * NT) + G * NT)
                            pe.wait_ge(v_done, s.batch(-1) + 1)
                            at_least(pe, out_copied, g)
                        last = pe.matmul(pv_ps[32 * j:32 * j + 32, :], V[i][:, t, p * G + j, :], P[p][j][:, t, :],
                                         start=(t == 0), stop=(t == NT - 1))
                        if k == G * NT + 1:
                            last.then_inc(pv_done, 1)
            run_steps(pe, -2, 2, 122, 128, step)

        @block.scalar
        def _(act):
            def step(s):
                for k in range(G * NT):
                    if s.exists(0):
                        g, p = s.group(0), s.half(0)
                        if k == 0:
                            at_least(act, pv_done, g - 1)
                        act.wait_ge(scores_filled, g * (G * NT) + (k + 1))
                        act.activation(P[p][k // NT][:, k % NT, :], sc_ps[k % 2][:, :], ACT.Exp, scale=SCALE).then_inc(exp_done, 1)
                    if s.exists(-2) and k == 1:
                        g, p = s.group(-2), s.half(-2)
                        act.wait_ge(pv_done, g + 1)
                        at_least(act, out_stored[p], s.pair(-2) * 16)
                        act.activation(out_sb[:, p, :], pv_ps[:, :], ACT.Copy).then_inc(out_copied, 1)
                    if s.exists(-2) and k == 3:
                        g, p = s.group(-2), s.half(-2)
                        act.wait_ge(out_copied, g + 1)
                        act.dma_start(heads_out[g], out_sb[:, p, :]).then_inc(out_stored[p], 16)
                    if s.exists(1) and k == 5:
                        g, p = s.group(1), s.half(1)
                        act.wait_ge(max_turned, g + 1)
                        at_least(act, max_rows_in_Q[p], s.pair(1) * 32)
                        act.activation(max_rows[:, p, :], turn_ps[:, :], ACT.Copy).then_inc(max_rows_done, 1)
                    if s.exists(1) and k == 7:
                        g, p, i = s.group(1), s.half(1), s.slot(1)
                        act.wait_ge(max_rows_done, g + 1)
                        for t in range(2):
                            act.dma_start(Q[i][KROW + t:KROW + t + 1, p * G:(p + 1) * G, :],
                                          max_rows[t * G * NT:(t + 1) * G * NT, p, :]).then_inc(max_rows_in_Q[p], 16)
            run_steps(act, -1, 4, 124, 129, step)


ROUND = 1.5 * 2.0 ** 23


class At:

    def __init__(self, turn, k, n):
        self.turn, self.k, self.n = turn, k, n

    def exists(self, back):
        return not isinstance(self.turn, int) or 0 <= self.k - back < self.n

    def batch(self, back):
        return self.turn * 8 + (self.k - back)

    def slot(self, back, slots):
        return (self.k - back) % slots

    def lap(self, back, slots):
        return self.turn * (8 // slots) + (self.k - back) // slots


def pipeline(eng, n, depth, body):
    assert n % 8 == 0 and depth <= 8
    for k in range(8):
        body(At(0, k, n))
    with eng.Fori(0, n // 8 - 1) as turn:
        for k in range(8):
            body(At(turn, 8 + k, n))
    for k in range(n, n + depth):
        body(At(0, k, n))


def prepare_ffn(nc, st, w_upT, w_downT, heads_out, recips):
    KU, KD = w_upT.shape[0] // 128, w_downT.shape[0] // 128
    NU, ND = w_upT.shape[1], w_downT.shape[1]
    N = KU * NU
    assert N == KD * ND
    B = recips.shape[0]
    CH = 8
    rows = heads_out.rearrange("(b g) (j r) m -> b (g j) r m", g=2, r=32)
    up = st.enter_context(nc.sbuf_tensor("w_up_ternary", [128, KU, NU], BF16))
    down = st.enter_context(nc.sbuf_tensor("w_down_ternary", [128, KD, ND], BF16))
    scale127 = st.enter_context(nc.sbuf_tensor("w_scale127", [128, 2], F32))
    with ExitStack() as tmp:
        sem = Semaphores(nc, "w_", tmp)
        w = [tmp.enter_context(nc.sbuf_tensor(f"w_in{i}", [128, N], F32)) for i in range(2)]
        ones = tmp.enter_context(nc.sbuf_tensor("w_ones", [128, 128], F32))
        sums = tmp.enter_context(nc.sbuf_tensor("w_sums", [128, 2], F32))
        scale = tmp.enter_context(nc.sbuf_tensor("w_scale", [128, 2], F32))
        inv = tmp.enter_context(nc.sbuf_tensor("w_inv", [128, 2], F32))
        total = tmp.enter_context(nc.psum_tensor("w_total", [128, 2], F32))
        loaded = [sem(f"loaded{i}") for i in range(2)]
        softmax_sums = tmp.enter_context(nc.sbuf_tensor("w_softmax_sums", [128, B, 32], F32))
        recip = tmp.enter_context(nc.sbuf_tensor("w_recip", [128, B, 32], F32))
        sums_loaded = [sem(f"sums_loaded{i}") for i in range(B // CH)]
        recip_done, recips_stored = sem("recip_done"), sem("recips_stored")
        chain, totalled, rounded, out = map(sem, ("chain", "totalled", "rounded", "out"))
        block = tmp.enter_context(nc.Block())
        views = [w[0][:, :].rearrange("p (k n) -> p k n", k=KU), w[1][:, :].rearrange("p (k n) -> p k n", k=KD)]

        @block.sync
        def _(sp):
            sp.dma_start(views[0], w_upT.rearrange("(k p) n -> p k n", p=128)).then_inc(loaded[0], 16)
            sp.dma_start(views[1], w_downT.rearrange("(k p) n -> p k n", p=128)).then_inc(loaded[1], 16)
            for c in range(B // CH):
                for b in range(c * CH, (c + 1) * CH):
                    sp.dma_start(softmax_sums[:, b, :], rows[b, :, 16, :].rearrange("h (p m) -> h p m", m=32)).then_inc(sums_loaded[c], 16)
            for c in range(B // CH):
                sp.wait_ge(recip_done, c + 1)
                sp.dma_start(recips[c * CH:(c + 1) * CH].rearrange("b p m -> p b m"), recip[:, c * CH:(c + 1) * CH, :]).then_inc(recips_stored, 16)
            sp.wait_ge(recips_stored, 16 * (B // CH))

        @block.vector
        def _(dve):
            n = [0]

            def link(ins):
                n[0] += 1
                ins.then_inc(chain, 1)
                dve.wait_ge(chain, n[0])
            link(dve.memset(ones[:, :], 1.0))
            for i in range(2):
                dve.wait_ge(loaded[i], 16)
                link(dve.tensor_reduce(sums[:, i:i + 1], w[i][:, :], AX.X, ALU.add, apply_absolute_value=True))
            dve.wait_ge(totalled, 1)
            link(dve.tensor_scalar(scale[:, :], total[:, :], 1.0 / (128 * N), 1e-5, ALU.mult, ALU.max))
            link(dve.reciprocal(inv[:, :], scale[:, :]))
            link(dve.tensor_scalar(scale127[:, :], scale[:, :], 1.0 / 127.0, None, ALU.mult))
            for i in range(2):
                link(dve.tensor_scalar(w[i][:, :], w[i][:, :], inv[:, i:i + 1], ROUND, ALU.mult, ALU.add))
                dve.tensor_scalar(w[i][:, :], w[i][:, :], ROUND - 1.0, ROUND + 1.0, ALU.max, ALU.min).then_inc(rounded, 1)
            for c in range(B // CH):
                dve.wait_ge(sums_loaded[c], 16 * CH)
                dve.reciprocal(recip[:, c * CH:(c + 1) * CH, :], softmax_sums[:, c * CH:(c + 1) * CH, :]).then_inc(recip_done, 1)

        @block.tensor
        def _(pe):
            pe.wait_ge(chain, 3)
            pe.matmul(total[:, :], ones[:, :], sums[:, :], start=True, stop=True).then_inc(totalled, 1)

        @block.scalar
        def _(act):
            for i, (dst, src) in enumerate(((up, views[0]), (down, views[1]))):
                act.wait_ge(rounded, i + 1)
                act.activation(dst[:, :, :], src, ACT.Copy, bias=-ROUND).then_inc(out, 1)
            act.wait_ge(out, 2)
    return up, down, scale127


def ternary_ffn(nc, x, heads_out, recips, hadamard, ident, w_upT, w_downT, x_out):
    B, T, C = x.shape
    CK = C // 128
    I = w_upT.shape[1]
    IK = I // 128
    C1 = float(C) ** -0.5
    EPS = 1e-5
    rows = heads_out.rearrange("(b g) (j r) m -> b (g j) r m", g=2, r=32)

    with ExitStack() as st:
        up, down, scale127 = prepare_ffn(nc, st, w_upT, w_downT, heads_out, recips)

        def sb(name, shape, dt):
            return st.enter_context(nc.sbuf_tensor("b_" + name, shape, dt))

        sem = Semaphores(nc, "b_", st)

        x_in, o_in, r_in = sb("x_in", [128, 2, C], F32), sb("o_in", [128, 2, C], F32), sb("r_in", [128, 2, C], F32)
        scaled = sb("scaled", [128, C], F32)
        x1 = sb("x1", [128, 8, C], F32)
        stats, mean_var = sb("stats", [128, 6], F32), sb("mean_var", [128, 2, 2], F32)
        var_eps, rstd = sb("var_eps", [128, 1], F32), sb("rstd", [128, 2], F32)
        neg_half, neg_one = sb("neg_half", [128, 1], F32), sb("neg_one", [128, 1], F32)
        z, za, zb = sb("z", [128, 2, C], F32), sb("za", [128, C], F32), sb("zb", [128, 2, C], F32)
        zT = [sb(f"zT{i}", [128, CK, 128], F32) for i in range(2)]
        amax1, amax2 = sb("amax1", [128, 2], F32), sb("amax2", [128, 2], F32)
        s1, inv1, mul1 = sb("s1", [128, 4], F32), sb("inv1", [128, 1], F32), sb("mul1", [128, 2], F32)
        h_scale, kappa = sb("h_scale", [128, 1], F32), sb("kappa", [128, 1], F32)
        s2, inv2, mul2, out_mul = sb("s2", [128, 2], F32), sb("inv2", [128, 1], F32), sb("mul2", [128, 2], F32), sb("out_mul", [128, 4], F32)
        rnd1, q1 = sb("rnd1", [128, C], F32), sb("q1", [128, 2, C], BF16)
        q1T = [sb(f"q1T{i}", [128, CK, 128], BF16) for i in range(2)]
        relu, sq = sb("relu", [128, I], F32), sb("sq", [128, 2, I], F32)
        ua = sb("ua", [128, I], F32)
        u = [sb(f"u{i}", [128, IK, 128], F32) for i in range(2)]
        rnd2, q2 = sb("rnd2", [128, I], F32), sb("q2", [128, 2, I], BF16)
        q2T = [sb(f"q2T{i}", [128, IK, 128], BF16) for i in range(2)]
        x2 = sb("x2", [128, 2, C], F32)
        had = sb("had", [128, 384], F32)
        identf, identb = sb("identf", [128, 128], F32), sb("identb", [128, 128], BF16)

        def ps(name, shape, dt):
            return st.enter_context(nc.psum_tensor("b_" + name, shape, dt))
        zT_ps, t1_ps = ps("zT_ps", [128, CK, 128], F32), ps("t1_ps", [128, C], F32)
        qT_ps, hT_ps = ps("qT_ps", [128, IK, 128], BF16), ps("hT_ps", [128, IK, 128], F32)
        t2_ps, out_ps = ps("t2_ps", [128, I], F32), ps("out_ps", [128, C], F32)
        const_in, const_ready = sem("const_in"), sem("const_ready")
        x_loaded, o_loaded, r_loaded = ([sem(f"{n}_loaded{i}") for i in range(2)] for n in "xor")
        x2_stored = [sem(f"x2_stored{i}") for i in range(2)]
        (preset, scaled_done, x1_done, stats_done, moments_done, eps_done, rstd_done, z_done, za_done, zb_done) = map(
            sem, ("preset", "scaled_done", "x1_done", "stats_done", "moments_done", "eps_done", "rstd_done", "z_done", "za_done", "zb_done"))
        (zT_filled, zT_done, t1_filled, amax1_done, s1_done, inv1_done, mul1_done, rnd1_done, q1_done, q1T_filled, q1T_done) = map(
            sem, ("zT_filled", "zT_done", "t1_filled", "amax1_done", "s1_done", "inv1_done", "mul1_done", "rnd1_done", "q1_done",
                  "q1T_filled", "q1T_done"))
        (h_scale_done, kappa_done, hT_filled, relu_done, sq_done, ua_done, u_done, t2_filled, amax2_done, s2_done, inv2_done,
         mul2_done) = map(sem, ("h_scale_done", "kappa_done", "hT_filled", "relu_done", "sq_done", "ua_done", "u_done", "t2_filled",
                                "amax2_done", "s2_done", "inv2_done", "mul2_done"))
        (out_mul_done, rnd2_done, q2_done, q2T_filled, q2T_done, out_filled, x2_done, pool_passed, dve_passed, sp_passed) = map(
            sem, ("out_mul_done", "rnd2_done", "q2_done", "q2T_filled", "q2T_done", "out_filled", "x2_done", "pool_passed", "dve_passed", "sp_passed"))
        block = st.enter_context(nc.Block())

        @block.sync
        def _(sp):
            sp.dma_start(identf[:, :], ident).then_inc(const_in, 16)
            sp.dma_start(had[:, 0:128], hadamard).then_inc(const_in, 16)
            held = Held(sp, sp_passed)

            def step(t):
                if t.exists(0):
                    b, i = t.batch(0), t.slot(0, 2)
                    at_least(held, x1_done, b - 1)
                    sp.dma_start(x_in[:, i, :], x[b]).then_inc(x_loaded[i], 16)
                    sp.dma_start(o_in[:, i, :], rows[b, :, 0:16, :]).then_inc(o_loaded[i], 16)
                    sp.dma_start(r_in[:, i, :], recips[b].rearrange("(h o p) m -> h o (p m)", h=8, o=1).to_broadcast([8, 16, 512])).then_inc(r_loaded[i], 16)
                if t.exists(6):
                    b, i = t.batch(6), t.slot(6, 2)
                    held.wait_ge(x2_done, b + 1)
                    sp.dma_start(x_out[b], x2[:, i, :]).then_inc(x2_stored[i], 16)
            pipeline(sp, B, 7, step)
            for i in range(2):
                sp.wait_ge(x2_stored[i], 16 * B // 2)

        @block.gpsimd
        def _(pool):
            pool.memset(neg_half[:, :], -0.5).then_inc(preset, 1)
            pool.wait_ge(preset, 1)
            pool.memset(neg_one[:, :], -1.0).then_inc(preset, 1)
            pool.wait_ge(preset, 2)
            held = Held(pool, pool_passed)

            def step(t):
                if t.exists(1):
                    b, i = t.batch(1), t.slot(1, 2)
                    held.wait_ge(z_done, b + 1)
                    at_least(held, zT_filled, b - 1)
                    zi = z[:, i].rearrange("p (a o d) -> p a o d", a=2, o=2)
                    zo = za[:, :].rearrange("p (a o d) -> p a o d", a=2, o=2)
                    pool.tensor_tensor(zo[:, :, 0], zi[:, :, 0], zi[:, :, 1], ALU.add).then_inc(za_done, 1)
                    held.wait_ge(za_done, b * 2 + 1)
                    pool.tensor_tensor(zo[:, :, 1], zi[:, :, 0], zi[:, :, 1], ALU.subtract).then_inc(za_done, 1)
                    held.wait_ge(za_done, b * 2 + 2)
                    h = C // 2
                    pool.tensor_tensor(zb[:, i, 0:h], za[:, 0:h], za[:, h:C], ALU.add).then_inc(zb_done, 1)
                    held.wait_ge(zb_done, b * 2 + 1)
                    pool.tensor_tensor(zb[:, i, h:C], za[:, 0:h], za[:, h:C], ALU.subtract).then_inc(zb_done, 1)
                    held.wait_ge(zb_done, b * 2 + 2)
                if t.exists(0):
                    b, i, j = t.batch(0), t.slot(0, 2), t.slot(0, 8)
                    held.wait_ge(o_loaded[i], t.lap(0, 2) * 16 + 16)
                    held.wait_ge(r_loaded[i], t.lap(0, 2) * 16 + 16)
                    pool.tensor_tensor(scaled[:, :], o_in[:, i, :], r_in[:, i, :], ALU.mult).then_inc(scaled_done, 1)
                    held.wait_ge(scaled_done, b + 1)
                    held.wait_ge(x_loaded[i], t.lap(0, 2) * 16 + 16)
                    at_least(held, x2_done, b - 7)
                    pool.tensor_tensor(x1[:, j, :], x_in[:, i, :], scaled[:, :], ALU.add).then_inc(x1_done, 1)
                    held.wait_ge(x1_done, b + 1)
                    held.wait_ge(moments_done, b + 1)
                    pool.tensor_scalar(var_eps[:, :], mean_var[:, i, 1:2], 1.0, EPS, ALU.mult, ALU.add).then_inc(eps_done, 1)
                    held.wait_ge(eps_done, b + 1)
                    at_least(held, z_done, b - 1)
                    pool.tensor_tensor(rstd[:, i:i + 1], var_eps[:, :], neg_half[:, :], ALU.pow).then_inc(rstd_done, 1)
                    held.wait_ge(rstd_done, b + 1)
                if t.exists(4):
                    b, i = t.batch(4), t.slot(4, 2)
                    pool.tensor_scalar(h_scale[:, :], s1[:, t.slot(4, 4):t.slot(4, 4) + 1], scale127[:, 0:1], 1.0, ALU.mult, ALU.mult).then_inc(h_scale_done, 1)
                    held.wait_ge(h_scale_done, b + 1)
                    pool.tensor_scalar(kappa[:, :], h_scale[:, :], h_scale[:, 0:1], float(I) ** -0.5, ALU.mult, ALU.mult).then_inc(kappa_done, 1)
                    held.wait_ge(kappa_done, b + 1)
                    held.wait_ge(amax2_done, b + 1)
                    pool.tensor_scalar(s2[:, i:i + 1], amax2[:, i:i + 1], kappa[:, 0:1], 1e-5, ALU.mult, ALU.max).then_inc(s2_done, 1)
                    held.wait_ge(s2_done, b + 1)
                    pool.tensor_tensor(inv2[:, :], s2[:, i:i + 1], neg_one[:, :], ALU.pow).then_inc(inv2_done, 1)
                    held.wait_ge(inv2_done, b + 1)
                    at_least(held, rnd2_done, b - 1)
                    pool.tensor_scalar(mul2[:, i:i + 1], inv2[:, :], kappa[:, 0:1], 127.0, ALU.mult, ALU.mult).then_inc(mul2_done, 1)
                    held.wait_ge(mul2_done, b + 1)
                    at_least(held, x2_done, b - 3)
                    j = t.slot(4, 4)
                    pool.tensor_scalar(out_mul[:, j:j + 1], s2[:, i:i + 1], scale127[:, 1:2], 1.0, ALU.mult, ALU.mult).then_inc(out_mul_done, 1)
                    held.wait_ge(out_mul_done, b + 1)
                if t.exists(1):
                    b, i, j = t.batch(1), t.slot(1, 2), t.slot(1, 4)
                    held.wait_ge(amax1_done, b + 1)
                    pool.tensor_scalar(s1[:, j:j + 1], amax1[:, i:i + 1], C1, 1e-5, ALU.mult, ALU.max).then_inc(s1_done, 1)
                    held.wait_ge(s1_done, b + 1)
                    pool.tensor_tensor(inv1[:, :], s1[:, j:j + 1], neg_one[:, :], ALU.pow).then_inc(inv1_done, 1)
                    held.wait_ge(inv1_done, b + 1)
                    at_least(held, rnd1_done, b - 1)
                    pool.tensor_scalar(mul1[:, i:i + 1], inv1[:, :], 127.0 * C1, 0.0, ALU.mult, ALU.add).then_inc(mul1_done, 1)
                    held.wait_ge(mul1_done, b + 1)
            pipeline(pool, B, 7, step)

        @block.vector
        def _(dve):
            dve.wait_ge(const_in, 32)
            dve.tensor_copy(identb[:, :], identf[:, :]).then_inc(const_ready, 1)
            dve.tensor_copy(had[:, 128:256], had[:, 0:128]).then_inc(const_ready, 1)
            dve.tensor_scalar(had[:, 256:384], had[:, 0:128], -1.0, None, ALU.mult).then_inc(const_ready, 1)
            held = Held(dve, dve_passed)

            def step(t):
                if t.exists(4):
                    b, i = t.batch(4), t.slot(4, 2)
                    dve.wait_ge(sq_done, b + 1)
                    v = sq[:, i].rearrange("p (a o d) -> p a o d", a=2, o=2)
                    w = ua[:, :].rearrange("p (a o d) -> p a o d", a=2, o=2)
                    dve.tensor_tensor(w[:, :, 0], v[:, :, 0], v[:, :, 1], ALU.add).then_inc(ua_done, 1)
                    dve.tensor_tensor(w[:, :, 1], v[:, :, 0], v[:, :, 1], ALU.subtract).then_inc(ua_done, 1)
                    dve.wait_ge(ua_done, b * 2 + 2)
                    at_least(dve, t2_filled, b - 1)
                    h = IK // 2
                    dve.tensor_tensor(u[i][:, 0:h].rearrange("p k d -> p (k d)"), ua[:, 0:I // 2], ua[:, I // 2:I], ALU.add).then_inc(u_done, 1)
                    dve.tensor_tensor(u[i][:, h:IK].rearrange("p k d -> p (k d)"), ua[:, 0:I // 2], ua[:, I // 2:I], ALU.subtract).then_inc(u_done, 1)
                    dve.wait_ge(u_done, b * 2 + 2)
                if t.exists(5):
                    b, i = t.batch(5), t.slot(5, 2)
                    dve.wait_ge(rnd2_done, b + 1)
                    at_least(dve, q2T_filled, b - 1)
                    dve.tensor_scalar(q2[:, i, :], rnd2[:, :], ROUND, None, ALU.subtract).then_inc(q2_done, 1)
                if t.exists(2):
                    b, i = t.batch(2), t.slot(2, 2)
                    dve.wait_ge(rnd1_done, b + 1)
                    at_least(dve, q1T_filled, b - 1)
                    dve.tensor_scalar(q1[:, i, :], rnd1[:, :], ROUND, None, ALU.subtract).then_inc(q1_done, 1)
                if t.exists(6):
                    b, i, j = t.batch(6), t.slot(6, 2), t.slot(6, 8)
                    dve.wait_ge(out_mul_done, b + 1)
                    dve.wait_ge(out_filled, b + 1)
                    at_least(dve, x2_stored[i], t.lap(6, 2) * 16)
                    jj = t.slot(6, 4)
                    dve.scalar_tensor_tensor(x2[:, i, :], out_ps[:, :], out_mul[:, jj:jj + 1], x1[:, j, :], ALU.mult, ALU.add).then_inc(x2_done, 1)
                if t.exists(2):
                    b, i = t.batch(2), t.slot(2, 2)
                    dve.wait_ge(q1T_filled, b + 1)
                    at_least(dve, hT_filled, b - 1)
                    dve.tensor_scalar(q1T[i][:, :, :], qT_ps[:, 0:CK, :], -127.0, 127.0, ALU.max, ALU.min).then_inc(q1T_done, 1)
                if t.exists(4):
                    b, i = t.batch(4), t.slot(4, 2)
                    dve.wait_ge(t2_filled, b + 1)
                    at_least(dve, s2_done, b - 1)
                    dve.tensor_reduce(amax2[:, i:i + 1], t2_ps[:, :], AX.X, ALU.max, apply_absolute_value=True).then_inc(amax2_done, 1)
                if t.exists(1):
                    b, i = t.batch(1), t.slot(1, 2)
                    dve.wait_ge(t1_filled, b + 1)
                    at_least(dve, s1_done, b - 1)
                    dve.tensor_reduce(amax1[:, i:i + 1], t1_ps[:, :], AX.X, ALU.max, apply_absolute_value=True).then_inc(amax1_done, 1)
                if t.exists(0):
                    b, i, j = t.batch(0), t.slot(0, 2), t.slot(0, 8)
                    dve.wait_ge(x1_done, b + 1)
                    dve.bn_stats(stats[:, :], x1[:, j, :]).then_inc(stats_done, 1)
                    at_least(held, z_done, b - 1)
                    held.wait_ge(stats_done, b + 1)
                    dve.bn_aggr(mean_var[:, i, :], stats[:, :]).then_inc(moments_done, 1)
                if t.exists(5):
                    b, i = t.batch(5), t.slot(5, 2)
                    dve.wait_ge(q2T_filled, b + 1)
                    at_least(dve, out_filled, b - 1)
                    dve.tensor_scalar(q2T[i][:, :, :], qT_ps[:, :, :], -127.0, 127.0, ALU.max, ALU.min).then_inc(q2T_done, 1)
                if t.exists(0):
                    b, i, j = t.batch(0), t.slot(0, 2), t.slot(0, 8)
                    dve.wait_ge(rstd_done, b + 1)
                    at_least(dve, za_done, b * 2 - 2)
                    dve.tensor_scalar(z[:, i, :], x1[:, j, :], mean_var[:, i, 0:1], rstd[:, i:i + 1], ALU.subtract, ALU.mult).then_inc(z_done, 1)
            pipeline(dve, B, 7, step)

        @block.tensor
        def _(pe):
            pe.wait_ge(const_ready, 3)

            def step(t):
                if t.exists(3):
                    b, i = t.batch(3), t.slot(3, 2)
                    pe.wait_ge(q1T_done, b + 1)
                    at_least(pe, relu_done, b)
                    for k in range(IK):
                        for c in range(CK):
                            last = pe.matmul(hT_ps[:, k, :], up[:, c, k * 128:(k + 1) * 128], q1T[i][:, c, :], start=(c == 0), stop=(c == CK - 1))
                    last.then_inc(hT_filled, 1)
                if t.exists(6):
                    b, i = t.batch(6), t.slot(6, 2)
                    pe.wait_ge(q2T_done, b + 1)
                    at_least(pe, x2_done, b)
                    for k in range(IK):
                        last = pe.matmul(out_ps[:, :], q2T[i][:, k, :], down[:, k, :], start=(k == 0), stop=(k == IK - 1))
                    last.then_inc(out_filled, 1)
                if t.exists(4):
                    b, i = t.batch(4), t.slot(4, 2)
                    pe.wait_ge(u_done, b * 2 + 2)
                    at_least(pe, rnd2_done, b)
                    for k in range(0, IK, 2):
                        pe.matmul(t2_ps[:, k * 128:(k + 2) * 128], u[i][:, k, :], had[:, 0:256], start=True, stop=False)
                        last = pe.matmul(t2_ps[:, k * 128:(k + 2) * 128], u[i][:, k + 1, :], had[:, 128:384], start=False, stop=True)
                    last.then_inc(t2_filled, 1)
                if t.exists(1):
                    b, i = t.batch(1), t.slot(1, 2)
                    pe.wait_ge(zb_done, b * 2 + 2)
                    at_least(pe, zT_done, b)
                    for c in range(CK):
                        last = pe.transpose(zT_ps[:, c, :], zb[:, i, c * 128:(c + 1) * 128], identf[:, :])
                    last.then_inc(zT_filled, 1)
                if t.exists(2):
                    b, i = t.batch(2), t.slot(2, 2)
                    pe.wait_ge(q1_done, b + 1)
                    at_least(pe, q2T_done, b - 3)
                    for c in range(CK):
                        last = pe.transpose(qT_ps[:, c, :], q1[:, i, c * 128:(c + 1) * 128], identb[:, :])
                    last.then_inc(q1T_filled, 1)
                if t.exists(1):
                    b, i = t.batch(1), t.slot(1, 2)
                    pe.wait_ge(zT_done, b + 1)
                    at_least(pe, rnd1_done, b)
                    for c in range(CK):
                        last = pe.matmul(t1_ps[:, c * 128:(c + 1) * 128], zT[i][:, c, :], had[:, 0:128], start=True, stop=True)
                    last.then_inc(t1_filled, 1)
                if t.exists(5):
                    b, i = t.batch(5), t.slot(5, 2)
                    pe.wait_ge(q2_done, b + 1)
                    pe.wait_ge(q1T_done, min(b + 4, B) if isinstance(b, int) else b + 4)
                    for k in range(IK):
                        last = pe.transpose(qT_ps[:, k, :], q2[:, i, k * 128:(k + 1) * 128], identb[:, :])
                    last.then_inc(q2T_filled, 1)
            pipeline(pe, B, 7, step)

        @block.scalar
        def _(act):
            def step(t):
                if t.exists(5):
                    b, i = t.batch(5), t.slot(5, 2)
                    act.wait_ge(mul2_done, b + 1)
                    at_least(act, q2_done, b)
                    act.activation(rnd2[:, :], t2_ps[:, :], ACT.Copy, scale=mul2[:, i:i + 1], bias=ROUND).then_inc(rnd2_done, 1)
                if t.exists(2):
                    b, i = t.batch(2), t.slot(2, 2)
                    act.wait_ge(mul1_done, b + 1)
                    at_least(act, q1_done, b)
                    act.activation(rnd1[:, :], t1_ps[:, :], ACT.Copy, scale=mul1[:, i:i + 1], bias=ROUND).then_inc(rnd1_done, 1)
                if t.exists(3):
                    b, i = t.batch(3), t.slot(3, 2)
                    act.wait_ge(hT_filled, b + 1)
                    at_least(act, sq_done, b)
                    act.activation(relu[:, :], hT_ps[:, :, :], ACT.Relu).then_inc(relu_done, 1)
                if t.exists(1):
                    b, i = t.batch(1), t.slot(1, 2)
                    act.wait_ge(zT_filled, b + 1)
                    at_least(act, t1_filled, b - 1)
                    act.activation(zT[i][:, :, :], zT_ps[:, :, :], ACT.Copy).then_inc(zT_done, 1)
                if t.exists(3):
                    b, i = t.batch(3), t.slot(3, 2)
                    act.wait_ge(relu_done, b + 1)
                    at_least(act, ua_done, b * 2 - 2)
                    act.activation(sq[:, i, :], relu[:, :], ACT.Square).then_inc(sq_done, 1)
            pipeline(act, B, 7, step)


def causal_attention(nc, x, ctx, ctxT, ident, after, causal_cols, x_out):
    B, T, C = x.shape
    H, D = 16, 32
    G = 128 // D
    CK = C // 128
    SCALE = float(D) ** -0.5
    EPS = 1e-5

    with ExitStack() as st:
        def sb(name, shape, dt):
            return st.enter_context(nc.sbuf_tensor("c_" + name, shape, dt))

        def ps(name, shape, dt):
            return st.enter_context(nc.psum_tensor("c_" + name, shape, dt))

        sem = Semaphores(nc, "c_", st)

        x_in = sb("x_in", [128, 8, C], F32)
        stats, mean_var = sb("stats", [128, 6], F32), sb("mean_var", [128, 2, 2], F32)
        var_eps, rstd, neg_half = sb("var_eps", [128, 1], F32), sb("rstd", [128, 2], F32), sb("neg_half", [128, 1], F32)
        z = sb("z", [128, 2, C], F32)
        qT = [sb(f"qT{i}", [128, CK, 128], F32) for i in range(2)]
        KD = [sb(f"KD{i}", [128, CK, G, 128], F32) for i in range(2)]
        V = [sb(f"V{i}", [128, C], F32) for i in range(4)]
        neg_max, bias = sb("neg_max", [128, 2, H], F32), sb("bias", [128, 2, H], F32)
        P = sb("P", [128, 2, H, 128], F32)
        sums = sb("sums", [128, 4, H], F32)
        masked = sb("masked", [128, 4, H], F32)
        total, recip = sb("total", [128, 4, H], F32), sb("recip", [128, 4, H], F32)
        PT = [sb(f"PT{i}", [128, H, 128], F32) for i in range(2)]
        oT = sb("oT", [128, 2, CK, 128], F32)
        masked_v, o_sum, o_norm = sb("masked_v", [128, C], F32), sb("o_sum", [128, 2, C], F32), sb("o_norm", [128, C], F32)
        x3 = sb("x3", [128, 2, C], F32)
        identf, identb = sb("identf", [128, 128], F32), sb("identb", [128, 128], BF16)
        after_sb, far = sb("after_sb", [128, 128], F32), sb("far", [128, 128], F32)
        farb = sb("farb", [128, 128], BF16)
        cols = sb("cols", [128, 3], F32)

        s_ps = ps("s_ps", [128, CK, G, 128], F32)
        pT_ps = [ps(f"pT_ps{i}", [128, G, 128], F32) for i in range(2)]
        bank_a, bank_b = ps("bank_a", [128, CK, 128], F32), ps("bank_b", [128, CK, 128], F32)

        const_in, const_ready, far_turned = sem("const_in"), sem("const_ready"), sem("far_turned")
        x_loaded = [sem(f"x_loaded{i}") for i in range(2)]
        k_loaded = [sem(f"k_loaded{i}") for i in range(2)]
        v_loaded = [sem(f"v_loaded{i}") for i in range(4)]
        x3_stored = [sem(f"x3_stored{i}") for i in range(2)]
        preset, stats_done, moments_done, eps_done, rstd_done, z_done = map(
            sem, ("preset", "stats_done", "moments_done", "eps_done", "rstd_done", "z_done"))
        qT_filled, qT_done, s_filled, max_done, bias_done, exp_done, masked_done = map(
            sem, ("qT_filled", "qT_done", "s_filled", "max_done", "bias_done", "exp_done", "masked_done"))
        pT_filled, pT_even_done, pT_odd_done, oT_filled, oT_done, o_filled, mv_filled = map(
            sem, ("pT_filled", "pT_even_done", "pT_odd_done", "oT_filled", "oT_done", "o_filled", "mv_filled"))
        total_done, recip_done, masked_v_done, o_sum_done, o_norm_done, x3_done = map(
            sem, ("total_done", "recip_done", "masked_v_done", "o_sum_done", "o_norm_done", "x3_done"))
        sp_passed, pool_passed, dve_passed = map(sem, ("sp_passed", "pool_passed", "dve_passed"))
        block = st.enter_context(nc.Block())

        @block.sync
        def _(sp):
            sp.dma_start(identf[:, :], ident).then_inc(const_in, 16)
            sp.dma_start(after_sb[:, :], after).then_inc(const_in, 16)
            sp.dma_start(cols[:, :], causal_cols).then_inc(const_in, 16)
            sp.wait_ge(preset, 3)
            held = Held(sp, sp_passed)

            def step(t):
                if t.exists(0):
                    b, j = t.batch(0), t.slot(0, 8)
                    at_least(held, x3_done, b - 7)
                    at_least(held, moments_done, b - 1)
                    sp.dma_start(x_in[:, j, :], x[b]).then_inc(x_loaded[t.slot(0, 2)], 16)
                    b, i = t.batch(0), t.slot(0, 2)
                    at_least(held, s_filled, (b - 1) * CK)
                    for h in range(G):
                        sp.dma_start(KD[i][h * D:(h + 1) * D, :, h, :],
                                     ctxT[b].rearrange("(c r) k -> r c k", r=128)[h * D:(h + 1) * D]).then_inc(k_loaded[i], 16)
                if t.exists(1):
                    b, i = t.batch(1), t.slot(1, 4)
                    at_least(held, oT_filled, b - 3)
                    sp.dma_start(V[i][:, :], ctx[b]).then_inc(v_loaded[i], 16)
                if t.exists(4):
                    b, i = t.batch(4), t.slot(4, 2)
                    held.wait_ge(x3_done, b + 1)
                    sp.dma_start(x_out[b], x3[:, i, :]).then_inc(x3_stored[i], 16)
            pipeline(sp, B, 5, step)
            for i in range(2):
                sp.wait_ge(x3_stored[i], 16 * B // 2)

        @block.gpsimd
        def _(pool):
            pool.memset(neg_half[:, :], -0.5).then_inc(preset, 1)
            pool.wait_ge(preset, 1)
            for i in range(2):
                pool.memset(KD[i][:, :, :, :], 0.0).then_inc(preset, 1)
                pool.wait_ge(preset, i + 2)
            held = Held(pool, pool_passed)

            def step(t):
                if t.exists(4):
                    b, i, j = t.batch(4), t.slot(4, 2), t.slot(4, 4)
                    held.wait_ge(o_sum_done, b + 1)
                    pool.tensor_tensor(o_norm[:, :].rearrange("p (h d) -> p h d", d=D), o_sum[:, i].rearrange("p (h d) -> p h d", d=D),
                                       recip[:, j].unsqueeze(2).to_broadcast([128, H, D]), ALU.mult).then_inc(o_norm_done, 1)
                    held.wait_ge(o_norm_done, b + 1)
                    at_least(held, x3_stored[i], t.lap(4, 2) * 16)
                    pool.tensor_tensor(x3[:, i, :], o_norm[:, :], x_in[:, t.slot(4, 8), :], ALU.add).then_inc(x3_done, 1)
                    held.wait_ge(x3_done, b + 1)
                if t.exists(0):
                    b, i = t.batch(0), t.slot(0, 2)
                    held.wait_ge(moments_done, b + 1)
                    pool.tensor_scalar(var_eps[:, :], mean_var[:, i, 1:2], 1.0, EPS, ALU.mult, ALU.add).then_inc(eps_done, 1)
                    held.wait_ge(eps_done, b + 1)
                    at_least(held, z_done, b - 1)
                    pool.tensor_tensor(rstd[:, i:i + 1], var_eps[:, :], neg_half[:, :], ALU.pow).then_inc(rstd_done, 1)
                    held.wait_ge(rstd_done, b + 1)
            pipeline(pool, B, 5, step)

        @block.vector
        def _(dve):
            dve.wait_ge(const_in, 48)
            dve.tensor_copy(identb[:, :], identf[:, :]).then_inc(const_ready, 1)
            dve.wait_ge(far_turned, 1)
            dve.tensor_scalar(farb[:, :], bank_a[:, 0, :], -2.0 ** 120, None, ALU.mult).then_inc(const_ready, 1)
            held = Held(dve, dve_passed)

            def step(t):
                for c in range(CK):
                    if t.exists(2):
                        b, i = t.batch(2), t.slot(2, 2)
                        dve.wait_ge(s_filled, b * CK + c + 1)
                        dve.tensor_reduce(neg_max[:, i, c * G:(c + 1) * G], s_ps[:, c], AX.X, ALU.max, negate=True).then_inc(max_done, 1)
                        dve.wait_ge(max_done, b * CK + c + 1)
                        if c == 0:
                            at_least(dve, masked_done, b - 1)
                        dve.tensor_scalar(bias[:, i, c * G:(c + 1) * G], neg_max[:, i, c * G:(c + 1) * G], cols[:, 0:1], SCALE,
                                          ALU.min, ALU.mult).then_inc(bias_done, 1)
                    if t.exists(4) and c == 0:
                        b, i, j = t.batch(4), t.slot(4, 2), t.slot(4, 4)
                        dve.wait_ge(masked_done, b + 1)
                        dve.scalar_tensor_tensor(total[:, j, :], masked[:, j, :], cols[:, 2:3], sums[:, j, :], ALU.mult, ALU.add).then_inc(total_done, 1)
                        dve.wait_ge(total_done, b + 1)
                        at_least(dve, o_norm_done, b - 3)
                        dve.reciprocal(recip[:, j, :], total[:, j, :]).then_inc(recip_done, 1)
                        dve.wait_ge(recip_done, b + 1)
                        dve.wait_ge(o_filled, b + 1)
                        dve.wait_ge(masked_v_done, b + 1)
                        at_least(dve, o_norm_done, b - 1)
                        dve.tensor_tensor(o_sum[:, i, :], bank_b[:, :, :].rearrange("p c d -> p (c d)"), masked_v[:, :], ALU.add).then_inc(o_sum_done, 1)
                    if t.exists(3) and c % 2 == 0:
                        b, i = t.batch(3), t.slot(3, 2)
                        dve.wait_ge(pT_filled, b * CK + c + 1)
                        dve.tensor_copy(PT[i][:, c * G:(c + 1) * G, :], pT_ps[0][:, :, :]).then_inc(pT_even_done, 1)
                    if t.exists(3) and c == 2:
                        b, j = t.batch(3), t.slot(3, 4)
                        dve.wait_ge(masked_done, b + 1)
                        dve.wait_ge(mv_filled, b + 1)
                        at_least(dve, o_sum_done, b)
                        dve.tensor_tensor(masked_v[:, :].rearrange("p (h d) -> p h d", d=D), bank_a[:, :, :].rearrange("p c (g d) -> p (c g) d", d=D),
                                          masked[:, j].unsqueeze(2).to_broadcast([128, H, D]), ALU.mult).then_inc(masked_v_done, 1)
                    if t.exists(1) and c == 0:
                        b, i, j = t.batch(1), t.slot(1, 2), t.slot(1, 8)
                        dve.wait_ge(rstd_done, b + 1)
                        at_least(dve, qT_filled, b - 1)
                        dve.tensor_scalar(z[:, i, :], x_in[:, j, :], mean_var[:, i, 0:1], rstd[:, i:i + 1], ALU.subtract, ALU.mult).then_inc(z_done, 1)
                    if t.exists(0) and c == 1:
                        b, i, j = t.batch(0), t.slot(0, 2), t.slot(0, 8)
                        dve.wait_ge(x_loaded[i], t.lap(0, 2) * 16 + 16)
                        dve.bn_stats(stats[:, :], x_in[:, j, :]).then_inc(stats_done, 1)
                        at_least(held, z_done, b - 1)
                        held.wait_ge(stats_done, b + 1)
                        dve.bn_aggr(mean_var[:, i, :], stats[:, :]).then_inc(moments_done, 1)
            pipeline(dve, B, 5, step)

        @block.tensor
        def _(pe):
            pe.wait_ge(const_in, 48)
            pe.transpose(bank_a[:, 0, :], after_sb[:, :], identf[:, :]).then_inc(far_turned, 1)
            pe.wait_ge(const_ready, 2)

            def step(t):
                for c in range(CK):
                    if t.exists(2):
                        b, i = t.batch(2), t.slot(2, 2)
                        if c == 0:
                            pe.wait_ge(k_loaded[i], t.lap(2, 2) * 64 + 64)
                            pe.wait_ge(qT_done, b + 1)
                        at_least(pe, exp_done, (b - 1) * H + (c + 1) * G)
                        pe.matmul(s_ps[:, c], qT[i][:, c, :], KD[i][:, c], start=True, stop=False)
                        pe.matmul(s_ps[:, c], identb[:, :], farb[:, :].unsqueeze(1).to_broadcast([128, G, 128]),
                                  start=False, stop=True).then_inc(s_filled, 1)
                    if t.exists(4) and c == 0:
                        b, i = t.batch(4), t.slot(4, 2)
                        pe.wait_ge(oT_done, b + 1)
                        for k in range(CK):
                            last = pe.transpose(bank_b[:, k, :], oT[:, i, k, :], identf[:, :])
                        last.then_inc(o_filled, 1)
                    if t.exists(3):
                        b, i = t.batch(3), t.slot(3, 2)
                        pe.wait_ge(exp_done, b * H + (c + 1) * G)
                        at_least(pe, (pT_even_done, pT_odd_done)[c % 2], b * 2 + c // 2)
                        for g in range(G):
                            last = pe.transpose(pT_ps[c % 2][:, g, :], P[:, i, c * G + g, :], identf[:, :])
                        last.then_inc(pT_filled, 1)
                        if c > 0:
                            products(t, c - 1)
                        if c == 1:
                            pe.wait_ge(qT_done, min(b + 2, B) if isinstance(b, int) else b + 2)
                            pe.matmul(bank_a[:, :, :], after_sb[:, :], V[t.slot(3, 4)][:, :], start=True, stop=True).then_inc(mv_filled, 1)
                if t.exists(1):
                    b, i = t.batch(1), t.slot(1, 2)
                    pe.wait_ge(z_done, b + 1)
                    at_least(pe, masked_v_done, b - 1)
                    for c in range(CK):
                        last = pe.transpose(bank_a[:, c, :], z[:, i, c * 128:(c + 1) * 128], identf[:, :])
                    last.then_inc(qT_filled, 1)
                if t.exists(3):
                    products(t, CK - 1)

            def products(t, c):
                b, i = t.batch(3), t.slot(3, 2)
                if c == 0:
                    pe.wait_ge(v_loaded[t.slot(3, 4)], t.lap(3, 4) * 16 + 16)
                    at_least(pe, o_sum_done, b)
                pe.wait_ge((pT_even_done, pT_odd_done)[c % 2], b * 2 + c // 2 + 1)
                for g in range(G):
                    h = c * G + g
                    last = pe.matmul(bank_b[g * D:(g + 1) * D, c, :], V[t.slot(3, 4)][:, h * D:(h + 1) * D], PT[i][:, h, :],
                                     start=True, stop=True)
                if c == CK - 1:
                    last.then_inc(oT_filled, 1)
            pipeline(pe, B, 5, step)

        @block.scalar
        def _(act):
            act.wait_ge(const_in, 48)

            def step(t):
                for c in range(CK):
                    if t.exists(3) and c % 2 == 1:
                        b, i = t.batch(3), t.slot(3, 2)
                        act.wait_ge(pT_filled, b * CK + c + 1)
                        act.activation(PT[i][:, c * G:(c + 1) * G, :], pT_ps[1][:, :, :], ACT.Copy).then_inc(pT_odd_done, 1)
                    if t.exists(1) and c == CK - 1:
                        b, i = t.batch(1), t.slot(1, 2)
                        act.wait_ge(qT_filled, b + 1)
                        at_least(act, s_filled, (b - 1) * CK)
                        act.activation(qT[i][:, :, :], bank_a[:, :, :], ACT.Copy).then_inc(qT_done, 1)
                    if t.exists(2):
                        b, i = t.batch(2), t.slot(2, 2)
                        act.wait_ge(bias_done, b * CK + c + 1)
                        if c == 0:
                            at_least(act, pT_filled, (b - 1) * CK)
                            at_least(act, total_done, b - 3)
                        for g in range(G):
                            h = c * G + g
                            act.activation(P[:, i, h, :], s_ps[:, c, g, :], ACT.Exp, scale=SCALE, bias=bias[:, i, h:h + 1],
                                           accum_out=sums[:, t.slot(2, 4), h:h + 1]).then_inc(exp_done, 1)
                        if c == CK - 1:
                            at_least(act, masked_v_done, b - 3)
                            act.activation(masked[:, t.slot(2, 4), :], bias[:, i, :], ACT.Exp, bias=cols[:, 1:2]).then_inc(masked_done, 1)
                if t.exists(3):
                    b, i = t.batch(3), t.slot(3, 2)
                    act.wait_ge(oT_filled, b + 1)
                    at_least(act, o_filled, b - 1)
                    act.activation(oT[:, i], bank_b[:, :, :], ACT.Copy).then_inc(oT_done, 1)
            pipeline(act, B, 5, step)


class Unit:

    UNITS = 16

    def __init__(self, q, k, back):
        self.q, self.k = q, k - back

    def exists(self):
        return not isinstance(self.q, int) or 0 <= self.k < self.UNITS

    def n(self):
        return self.q * 4 + self.k

    def pair(self):
        return self.k % 2

    def second(self):
        return self.k % 4 >= 2

    def turn(self):
        return self.q + self.k // 4

    def eight(self):
        return self.turn() * 2 + self.pair()


def units(eng, body):
    for k in range(2):
        body(Unit(0, k, 0), Unit(0, k, 1))
    with eng.Fori(0, 3) as q:
        for k in range(2, 6):
            body(Unit(q, k, 0), Unit(q, k, 1))
    for k in range(14, 17):
        body(Unit(0, k, 0), Unit(0, k, 1))


def workspace_ffn(nc, x, ident, workspace, compete_wT, compete_b, write_wT, write_b, wq, wkT, wvT, in_proj_cols,
                  out_wT, out_b, pre_cols, norm_post, x_out):
    B, T, C = x.shape
    S, K, H = 16, 4, 8
    D = C // H
    CK = C // 128
    NB = 8
    EPS, NORM_EPS = 1e-6, 1e-5
    SCALE = float(D) ** -0.5
    FAR = 3.0e38

    with ExitStack() as st:
        def sb(name, shape, dt=F32):
            return st.enter_context(nc.sbuf_tensor("d_" + name, shape, dt))

        def ps(name, shape, dt=F32):
            return st.enter_context(nc.psum_tensor("d_" + name, shape, dt))

        sem = Semaphores(nc, "d_", st)

        identf = sb("identf", [128, 128])
        cw_in, cw = sb("cw_in", [128, CK, S]), sb("cw", [128, CK, 2 * S])
        pre_col, cb_col = sb("pre_col", [128, CK]), sb("cb_col", [128, 1])
        write_sb, wk_sb, wv_sb, wq_sb, wo_sb = (sb(n, [128, CK, C]) for n in ("write_sb", "wk_sb", "wv_sb", "wq_sb", "wo_sb"))
        bias_cols = sb("bias_cols", [128, 3, CK])
        bq_wide = sb("bq_wide", [128, CK, 128])
        write_b_row, out_b_row, post_row = sb("write_b_row", [128, C]), sb("out_b_row", [128, C]), sb("post_row", [128, C])
        ws_first = sb("ws_first", [128, C])
        neg_half = sb("neg_half", [128, NB])

        X = [sb(f"X{i}", [128, NB, C]) for i in range(2)]
        XT = [sb(f"XT{i}", [128, CK, NB, 128]) for i in range(2)]
        junk, x_sq, x_ms, x_r = sb("junk", [128, C], BF16), sb("x_sq", [128, NB]), sb("x_ms", [128, NB]), sb("x_r", [128, NB])
        stats, moments = sb("stats", [128, NB, 6]), sb("moments", [128, NB, 2])
        var_eps, rstd = sb("var_eps", [128, NB]), sb("rstd", [128, NB])
        lt = sb("lt", [128, 512])
        lr = sb("lr", [128, NB, S])
        lg, lg_out = sb("lg", [128, 136]), sb("lg_out", [128, 136])
        top, chosen, neg_top = sb("top", [128, 8]), sb("chosen", [128, 8]), sb("neg_top", [128, 1])
        is_top, e_top, w_raw, w_top = sb("is_top", [128, 128]), sb("e_top", [128, 128]), sb("w_raw", [128, 128]), sb("w_top", [128, 128])
        w_sum, w_inv = sb("w_sum", [128, 1]), sb("w_inv", [128, 1])
        WT = sb("WT", [128, NB, 2 * S])
        g = sb("g", [128, 2, C])
        gT = sb("gT", [128, CK, NB, S])
        ws_sum, ws_sq, ws_ms, ws_r = sb("ws_sum", [128, C]), sb("ws_sq", [128, 1]), sb("ws_ms", [128, 1]), sb("ws_r", [128, 1])
        junk2 = sb("junk2", [128, C], BF16)
        ws = [sb(f"ws{i}", [128, C]) for i in range(2)]
        ws_base = [sb(f"ws_base{i}", [128, C]) for i in range(2)]
        ws_in = ws_base[0]
        wsT = sb("wsT", [128, CK, 128])
        kd, vd = sb("kd", [128, CK, NB, 2, S]), [sb(f"vd{i}", [128, CK, NB, 2, S]) for i in range(2)]
        s_bias = sb("s_bias", [128, NB, CK, 2 * S])
        A = sb("A", [128, CK, NB, CK, 2 * S])
        sc = sb("sc", [128, 2, 512])
        sc_max, sc_exp = sb("sc_max", [128, 2, 32]), sb("sc_exp", [128, 2, 512])
        sc_sum, sc_inv = sb("sc_sum", [128, 2, 32]), sb("sc_inv", [128, 2, 32])
        att = sb("att", [128, 2, 512])
        attT = [sb(f"attT{i}", [128, NB // 2, 128]) for i in range(2)]
        VO = [sb(f"VO{i}", [128, C]) for i in range(2)]
        y, y_sq, y_ms, y_r = sb("y", [128, 2, C]), sb("y_sq", [128, 2]), sb("y_ms", [128, 1]), sb("y_r", [128, 2])
        x_first, out_sb = sb("x_first", [128, 2, C]), sb("out_sb", [128, 2, C])

        F = [ps(f"F{i}", [128, 512]) for i in range(3)]
        SC = [ps(f"SC{i}", [128, 512]) for i in range(2)]
        vo_ps = ps("vo_ps", [128, 512])
        xb_ps = [ps(f"xb_ps{i}", [128, 512]) for i in range(2)]

        small_in, big_in, const_ready, preset = sem("small_in"), sem("big_in"), sem("const_ready"), sem("preset")
        x_loaded = [sem(f"x_loaded{i}") for i in range(2)]
        out_stored = [sem(f"out_stored{i}") for i in range(2)]
        x_first_loaded = [sem(f"x_first_loaded{i}") for i in range(2)]
        out_ready = sem("out_ready")
        (xT_filled, xT_done, x_sq_done, x_ms_done, x_r_done, lt_filled, lt_done, l_filled, lr_done, lg_filled, lg_done) = map(
            sem, ("xT_filled", "xT_done", "x_sq_done", "x_ms_done", "x_r_done", "lt_filled", "lt_done", "l_filled", "lr_done",
                  "lg_filled", "lg_done"))
        (top_chain, e_top_done, w_top_done, wT_filled, wT_done, g_filled, g_done, gT_filled, gT_done, wr_filled, ws_sum_done) = map(
            sem, ("top_chain", "e_top_done", "w_top_done", "wT_filled", "wT_done", "g_filled", "g_done", "gT_filled", "gT_done",
                  "wr_filled", "ws_sum_done"))
        (ws_sq_done, ws_ms_done, ws_r_done, ws_done, ws_base_done, wsT_filled, wsT_done, kv_filled, kd_done, vd_done, bias_filled,
         bias_done, a_filled, a_done) = map(
            sem, ("ws_sq_done", "ws_ms_done", "ws_r_done", "ws_done", "ws_base_done", "wsT_filled", "wsT_done", "kv_filled",
                  "kd_done", "vd_done", "bias_filled", "bias_done", "a_filled", "a_done"))
        (sc_filled, sc_done, sc_max_done, sc_sub_done, sc_exp_done, sc_sum_done, sc_inv_done, att_done, attT_filled, attT_done) = map(
            sem, ("sc_filled", "sc_done", "sc_max_done", "sc_sub_done", "sc_exp_done", "sc_sum_done", "sc_inv_done", "att_done",
                  "attT_filled", "attT_done"))
        (vo_filled, vo_done, xb_filled, x_biased, y_done, y_sq_done, y_ms_done, y_r_done, final_done) = map(
            sem, ("vo_filled", "vo_done", "xb_filled", "x_biased", "y_done", "y_sq_done", "y_ms_done", "y_r_done", "final_done"))
        stats_done, moments_done, eps_done, rstd_done, z_done = map(sem, ("stats_done", "moments_done", "eps_done", "rstd_done", "z_done"))
        sp_passed, pool_passed, dve_passed = sem("sp_passed"), sem("pool_passed"), sem("dve_passed")
        block = st.enter_context(nc.Block())

        USES = ([(xT_done, NB, i) for i in range(NB)] + [(lt_done, 1, 0), (lr_done, 1, 0), (lg_done, 1, 0), (wT_done, 1, 0)]
                + [(g_done, 2, i) for i in range(2)] + [(gT_done, 2, i) for i in range(2)]
                + [(ws_sum_done, 1, 0), (wsT_done, 1, 0), (kd_done, 2, 1), (vd_done, 2, 1)]
                + [(bias_done, 2, i) for i in range(2)] + [(a_done, 2 * CK, i) for i in range(2 * CK)])
        (U_XT, U_LT, U_L, U_LG, U_WT, U_G, U_GT, U_WR, U_WST, U_K, U_V, U_BIAS, U_A) = (0, 8, 9, 10, 11, 12, 14, 16, 17, 18, 19, 20, 22)
        assert len(USES) % 3 == 0

        def bank(pe, u, use):
            if use >= 3:
                s, per, i = USES[use - 3]
                at_least(pe, s, u.n() * per + (i + 1))
            else:
                s, per, i = USES[use - 3 + len(USES)]
                at_least(pe, s, (u.n() - 1) * per + (i + 1))
            return F[use % 3]

        @block.sync
        def _(sp):
            for dst, src in ((identf[:, :], ident), (cw_in[:, :, :], compete_wT.rearrange("(c p) s -> p c s", p=128)),
                             (pre_col[:, :], pre_cols),
                             (bias_cols[:, :, :], in_proj_cols)):
                sp.dma_start(dst, src).then_inc(small_in, 16)
            for i in range(NB):
                sp.dma_start(cb_col[i * S:(i + 1) * S, :], compete_b.rearrange("(s o) -> s o", o=1)).then_inc(small_in, 16)
                sp.dma_start(ws_in[i * S:(i + 1) * S, :], workspace).then_inc(small_in, 16)
            for dst, src in ((write_b_row, write_b), (out_b_row, out_b), (post_row, norm_post)):
                sp.dma_start(dst[:, :], src.rearrange("(o n) -> o n", o=1).to_broadcast([128, C])).then_inc(small_in, 16)
            for i in range(2):
                for b in range(NB):
                    sp.dma_start(X[i][:, b, :], x[i * NB + b]).then_inc(x_loaded[i], 16)
            for dst, src in ((write_sb, write_wT), (wk_sb, wkT), (wv_sb, wvT), (wq_sb, wq), (wo_sb, out_wT)):
                sp.dma_start(dst[:, :, :], src.rearrange("(c p) n -> p c n", p=128)).then_inc(big_in, 16)
            held = Held(sp, sp_passed)
            for i in range(2):
                sp.sem_inc(out_stored[i], 16)

            def step(f, u):
                if u.exists() and u.second():
                    i = u.pair()

                    def load_first(b):
                        sp.dma_start(x_first[:, b % 2, :], x[u.eight() * NB + b]).then_inc(x_first_loaded[b % 2], 16)
                    load_first(0)
                    load_first(1)
                    for b in range(NB):
                        held.wait_ge(out_ready, u.eight() * NB + (b + 1))
                        sp.dma_start(x_out[u.eight() * NB + b], out_sb[:, b % 2, :]).then_inc(out_stored[b % 2], 16)
                        if b + 2 < NB:
                            load_first(b + 2)
                        if not isinstance(u.q, int):
                            sp.dma_start(X[i][:, b, :], x[(u.eight() + 2) * NB + b]).then_inc(x_loaded[i], 16)
            units(sp, step)
            for i in range(2):
                sp.wait_ge(out_stored[i], 16 + 16 * B // 2)

        @block.gpsimd
        def _(pool):
            n = 0
            for dst, value in ((neg_half[:, :], -0.5), (cw[:, :, :], 0.0), (lt[64:128, :], 0.0), (lg[:, 128:136], -FAR), (chosen[:, :], -FAR), (WT[:, :, :], 0.0),
                               (kd[:, :, :, :, :], 0.0), (vd[0][:, :, :, :, :], 0.0), (vd[1][:, :, :, :, :], 0.0)):
                pool.memset(dst, value).then_inc(preset, 1)
                n += 1
                pool.wait_ge(preset, n)
            held = Held(pool, pool_passed)

            def rms(sq, ms, r, ms_done, r_done, count, cols):
                pool.tensor_scalar(ms, sq, 1.0 / C, EPS, ALU.mult, ALU.add).then_inc(ms_done, 1)
                held.wait_ge(ms_done, count)
                pool.tensor_tensor(r, ms, neg_half[:, 0:cols], ALU.pow).then_inc(r_done, 1)
                held.wait_ge(r_done, count)

            def step(f, u):
                if f.exists() and not f.second():
                    e = f.eight()
                    held.wait_ge(moments_done, e * NB + NB)
                    pool.tensor_scalar(var_eps[:, :], moments[:, :, 1], 1.0, NORM_EPS, ALU.mult, ALU.add).then_inc(eps_done, 1)
                    held.wait_ge(eps_done, e + 1)
                    at_least(held, z_done, e * NB)
                    pool.tensor_tensor(rstd[:, :], var_eps[:, :], neg_half[:, :], ALU.pow).then_inc(rstd_done, 1)
                    held.wait_ge(rstd_done, e + 1)
                if u.exists():
                    for half in range(2):
                        n = u.n()
                        held.wait_ge(sc_inv_done, n * 2 + (half + 1))
                        at_least(held, attT_filled, (n - 1) * 2 + (half + 1))
                        pool.tensor_tensor(att[:, half].rearrange("p (h s) -> p h s", s=S), sc_exp[:, half].rearrange("p (h s) -> p h s", s=S),
                                           sc_inv[:, half].unsqueeze(2).to_broadcast([128, 32, S]), ALU.mult).then_inc(att_done, 1)
                        held.wait_ge(att_done, n * 2 + (half + 1))
                    add_bias(u, 0)
                    add_bias(u, 1)
                if f.exists():
                    n = f.n()
                    held.wait_ge(x_sq_done, n * NB + NB)
                    at_least(held, lr_done, n)
                    rms(x_sq[:, :], x_ms[:, :], x_r[:, :], x_ms_done, x_r_done, n + 1, NB)
                for b in range(NB):
                    if u.exists() and b >= 2:
                        add_bias(u, b)
                    if u.exists() and b >= 1:
                        finish(u, b - 1)
                    if f.exists() and b == 5:
                        n = f.n()
                        held.wait_ge(ws_sq_done, n + 1)
                        rms(ws_sq[:, :], ws_ms[:, :], ws_r[:, :], ws_ms_done, ws_r_done, n + 1, 1)
                    if f.exists() and b == 6:
                        n = f.n()
                        held.wait_ge(ws_done, n + 1)
                        pool.tensor_tensor(ws_base[f.pair()][:, :], ws[f.pair()][:, :], write_b_row[:, :], ALU.add).then_inc(ws_base_done, 1)
                        held.wait_ge(ws_base_done, n + 1)
                if u.exists():
                    finish(u, NB - 1)
                    if u.second():
                        add_first(u, NB - 1)

            def add_bias(u, b):
                i, n = u.pair(), u.n()
                if b == 0:
                    at_least(held, gT_done, n * 2 + 2)
                    at_least(held, xT_done, n * NB + NB)
                    at_least(held, x_sq_done, n * NB + NB)
                    held.wait_ge(g_done, n * 2 + 2)
                pool.tensor_tensor(X[i][:, b, :], X[i][:, b, :], out_b_row[:, :], ALU.add).then_inc(x_biased, 1)
                held.wait_ge(x_biased, n * NB + (b + 1))

            def add_first(u, b):
                m = u.eight() * NB + b
                held.wait_ge(final_done, u.n() * NB + (b + 1))
                held.wait_ge(x_first_loaded[b % 2], (u.eight() * (NB // 2) + (b // 2 + 1)) * 16)
                pool.tensor_tensor(out_sb[:, b % 2, :], out_sb[:, b % 2, :], x_first[:, b % 2, :], ALU.add).then_inc(out_ready, 1)
                held.wait_ge(out_ready, m + 1)

            def finish(u, b):
                m = u.n() * NB + b
                held.wait_ge(y_sq_done, m + 1)
                at_least(held, final_done, m - 1)
                rms(y_sq[:, b % 2:b % 2 + 1], y_ms[:, :], y_r[:, b % 2:b % 2 + 1], y_ms_done, y_r_done, m + 1, 1)
                if u.second() and b >= 1:
                    add_first(u, b - 1)
            pool.wait_ge(small_in, 16 * (7 + 2 * NB))
            units(pool, step)

        @block.vector
        def _(dve):
            dve.wait_ge(small_in, 16 * (7 + 2 * NB))
            dve.wait_ge(preset, 9)
            dve.tensor_tensor(cw[:, :, 0:S], cw_in[:, :, :], pre_col[:, :].unsqueeze(2).to_broadcast([128, CK, S]), ALU.mult).then_inc(const_ready, 1)
            dve.tensor_tensor(ws_first[:, :], ws_in[:, :], write_b_row[:, :], ALU.add).then_inc(const_ready, 1)
            dve.tensor_copy(bq_wide[:, :, :], bias_cols[:, 0].unsqueeze(2).to_broadcast([128, CK, 128])).then_inc(const_ready, 1)
            dve.wait_ge(const_ready, 3)
            held = Held(dve, dve_passed)
            LINKS = 6

            def step(f, u):
                def link(k, ins):
                    ins.then_inc(top_chain, 1)
                    dve.wait_ge(top_chain, f.n() * LINKS + k)

                def softmax(half):
                    n = u.n()
                    h4 = lambda t: t[:, half].rearrange("p (h s) -> p h s", s=S)
                    wide = lambda t: t[:, half].unsqueeze(2).to_broadcast([128, 32, S])
                    dve.wait_ge(sc_filled, n * 2 + (half + 1))
                    dve.wait_ge(bias_done, n * 2 + 2)
                    dve.tensor_tensor(sc[:, half, :], SC[half][:, :], s_bias[:, half * 4:half * 4 + 4].rearrange("p b c s -> p (b c s)"),
                                      ALU.add).then_inc(sc_done, 1)
                    dve.wait_ge(sc_done, n * 2 + (half + 1))
                    dve.tensor_reduce(sc_max[:, half, :], h4(sc), AX.X, ALU.max).then_inc(sc_max_done, 1)
                    dve.wait_ge(sc_max_done, n * 2 + (half + 1))
                    dve.tensor_tensor(h4(sc), h4(sc), wide(sc_max), ALU.subtract).then_inc(sc_sub_done, 1)

                def softmax_sum(half):
                    n = u.n()
                    dve.wait_ge(sc_exp_done, n * 2 + (half + 1))
                    dve.tensor_reduce(sc_sum[:, half, :], sc_exp[:, half].rearrange("p (h s) -> p h s", s=S), AX.X, ALU.add).then_inc(sc_sum_done, 1)
                    dve.wait_ge(sc_sum_done, n * 2 + (half + 1))
                    at_least(dve, att_done, (n - 1) * 2 + (half + 1))
                    dve.reciprocal(sc_inv[:, half, :], sc_sum[:, half, :]).then_inc(sc_inv_done, 1)

                def residual(b):
                    m = u.n() * NB + b
                    dve.wait_ge(x_biased, m + 1)
                    dve.wait_ge(xb_filled, m + 1)
                    dve.wait_ge(final_done, m) if not (isinstance(m, int) and m == 0) else None
                    dve.tensor_tensor(y[:, b % 2, :], xb_ps[b % 2][:, :], X[u.pair()][:, b, :], ALU.add).then_inc(y_done, 1)

                def final(b):
                    m = u.n() * NB + b
                    dve.wait_ge(y_r_done, m + 1)
                    if u.second():
                        at_least(dve, out_stored[b % 2], u_stores(u) * 64 + (b // 2 * 16 + 16))
                        dst = out_sb[:, b % 2, :]
                    else:
                        dst = X[u.pair()][:, b, :]
                    dve.scalar_tensor_tensor(dst, y[:, b % 2, :], y_r[:, b % 2:b % 2 + 1], post_row[:, :], ALU.mult, ALU.mult).then_inc(final_done, 1)

                def u_stores(u):
                    return u.turn() * 2 + u.pair()

                first = f.exists() and not f.second()
                if first:
                    e = f.eight()
                    dve.wait_ge(x_loaded[f.pair()], f.turn() * 128 + 128)
                    at_least(dve, z_done, e * NB)
                    for b in range(NB):
                        dve.bn_stats(stats[:, b, :], X[f.pair()][:, b, :]).then_inc(stats_done, 1)
                    for b in range(NB):
                        held.wait_ge(stats_done, e * NB + (b + 1))
                        dve.bn_aggr(moments[:, b, :], stats[:, b, :]).then_inc(moments_done, 1)
                if u.exists():
                    softmax(0)
                if first:
                    dve.wait_ge(rstd_done, e + 1)
                    for b in range(NB):
                        dve.tensor_scalar(X[f.pair()][:, b, :], X[f.pair()][:, b, :], moments[:, b, 0:1], rstd[:, b:b + 1],
                                          ALU.subtract, ALU.mult).then_inc(z_done, 1)
                if u.exists():
                    softmax(1)
                    softmax_sum(0)
                    softmax_sum(1)
                if f.exists():
                    n = f.n()
                    dve.wait_ge(x_r_done, n + 1)
                    dve.wait_ge(l_filled, n + 1)
                    dve.tensor_tensor(lr[:, :, :].rearrange("p (h q) s -> p q h s", h=2),
                                      F[U_L % 3][:, :].rearrange("p (q r) -> p q r", q=4)[:, :, 0:64].rearrange("p q (h s) -> p q h s", h=2)[:, :, :, 0:S],
                                      x_r[:, :].rearrange("p (h q) -> p q h", h=2).unsqueeze(3).to_broadcast([128, 4, 2, S]),
                                      ALU.mult).then_inc(lr_done, 1)
                if u.exists():
                    residual(0)
                if f.exists():
                    n = f.n()
                    held.wait_ge(lg_filled, n + 1)
                    dve.tensor_scalar(lg[:, 0:128], F[U_LG % 3][:, 0:128], cb_col[:, :], None, ALU.add).then_inc(lg_done, 1)
                    held.wait_ge(lg_done, n + 1)
                    dve.max(top[:, :], lg[:, :]).then_inc(top_chain, 1)
                    held.wait_ge(top_chain, n * LINKS + 1)
                    link(2, dve.tensor_scalar(neg_top[:, :], top[:, 0:1], -1.0, None, ALU.mult))
                    dve.tensor_copy(chosen[:, 0:K], top[:, 0:K]).then_inc(top_chain, 1)
                    held.wait_ge(top_chain, n * LINKS + 3)
                    dve.match_replace(lg_out[:, :], chosen[:, :], lg[:, :], FAR).then_inc(top_chain, 1)
                    held.wait_ge(top_chain, n * LINKS + 4)
                    link(5, dve.tensor_tensor(is_top[:, :], lg_out[:, 0:128], lg[:, 0:128], ALU.not_equal))
                    dve.wait_ge(e_top_done, n + 1)
                    dve.scalar_tensor_tensor(w_raw[:, :], e_top[:, :], 1.0, is_top[:, :], ALU.mult, ALU.mult, accum_out=w_sum[:, :]).then_inc(top_chain, 1)
                    dve.wait_ge(top_chain, n * LINKS + 6)
                    dve.reciprocal(w_inv[:, :], w_sum[:, :]).then_inc(w_top_done, 1)
                    dve.wait_ge(w_top_done, n * 2 + 1)
                    dve.tensor_scalar(w_top[:, :], w_raw[:, :], w_inv[:, :], None, ALU.mult).then_inc(w_top_done, 1)
                if u.exists():
                    final(0)
                    residual(1)
                if f.exists():
                    dve.wait_ge(wT_filled, f.n() + 1)
                    dve.tensor_copy(WT[:, :, 0:S], F[U_WT % 3][:, 0:128].rearrange("p (b s) -> p b s", s=S)).then_inc(wT_done, 1)
                if u.exists():
                    final(1)
                    residual(2)
                    final(2)
                    residual(3)
                if f.exists():
                    for i in range(2):
                        dve.wait_ge(gT_filled, f.n() * 2 + (i + 1))
                        if i == 0:
                            at_least(dve, wr_filled, f.n())
                        dve.tensor_copy(gT[:, :, i * 4:i * 4 + 4, :],
                                        F[(U_GT + i) % 3][:, :].rearrange("p (c b s) -> p c b s", c=CK, b=4)[:, :, :, 0:S]).then_inc(gT_done, 1)
                if u.exists():
                    final(3)
                    residual(4)
                if f.exists():
                    n = f.n()
                    dve.wait_ge(wr_filled, n + 1)
                    base = ws_base[f.pair()] if f.second() else ws_first
                    if f.second():
                        dve.wait_ge(ws_base_done, n - 1)
                    at_least(dve, ws_done, n)
                    dve.tensor_tensor(ws_sum[:, :], F[U_WR % 3][:, :], base[:, :], ALU.add).then_inc(ws_sum_done, 1)
                if u.exists():
                    final(4)
                    residual(5)
                if f.exists():
                    n = f.n()
                    dve.wait_ge(ws_r_done, n + 1)
                    at_least(dve, ws_base_done, n - 1)
                    at_least(dve, wsT_filled, n - 1)
                    dve.wait_ge(ws_sum_done, n + 1)
                    dve.scalar_tensor_tensor(ws[f.pair()][:, :], ws_sum[:, :], ws_r[:, :], post_row[:, :], ALU.mult, ALU.mult).then_inc(ws_done, 1)
                if u.exists():
                    final(5)
                    residual(6)
                    final(6)
                    residual(7)
                if f.exists():
                    n = f.n()
                    for w, dst, use, done in ((1, kd, U_K, kd_done), (2, vd[f.pair()], U_V, vd_done)):
                        dve.wait_ge(kv_filled, n * 2 + w)
                        if w == 1:
                            at_least(dve, a_filled, n * 2 * CK)
                        else:
                            at_least(dve, vo_filled, (n - 1) * NB)
                        for h in range(2):
                            r = slice(h * D, (h + 1) * D)
                            dve.tensor_tensor(dst[r, :, :, h, :], F[use % 3][r, :].rearrange("p (c b s) -> p c b s", c=CK, s=S),
                                              bias_cols[r, w].unsqueeze(2).unsqueeze(3).to_broadcast([D, CK, NB, S]), ALU.add).then_inc(done, 1)
                if u.exists():
                    final(7)
            units(dve, step)

        @block.tensor
        def _(pe):
            pe.wait_ge(const_ready, 3)

            def step(f, u):
                def value_out(b):
                    m = u.n() * NB + b
                    at_least(pe, vo_done, m)
                    pe.wait_ge(vd_done, u.n() * 2 + 2)
                    for p in range(CK):
                        last = pe.matmul(vo_ps[p * 32:(p + 1) * 32, :], vd[u.pair()][:, p, b].rearrange("p h s -> p (h s)"), wo_sb[:, p, :],
                                         start=True, stop=True)
                    last.then_inc(vo_filled, 1)

                def mix(b):
                    m = u.n() * NB + b
                    pe.wait_ge(vo_done, m + 1)
                    pe.wait_ge(attT_done, u.n() * 2 + (b // 4 + 1))
                    at_least(pe, y_done, m - 1)
                    pe.matmul(xb_ps[b % 2][:, :], attT[b // 4][:, b % 4, :], VO[b % 2][:, :], start=True, stop=True).then_inc(xb_filled, 1)

                if u.exists():
                    n, i = u.n(), u.pair()
                    for half in range(2):
                        at_least(pe, attT_done, (n - 1) * 2 + (half + 1))
                        pe.wait_ge(a_done, n * 2 * CK + 2 * CK)
                        for b in range(half * 4, half * 4 + 4):
                            for c in range(CK):
                                last = pe.matmul(SC[half][:, b % 4 * 128:(b % 4 + 1) * 128], XT[i][:, c, b, :],
                                                 A[:, c, b].rearrange("p c s -> p (c s)"), start=(c == 0), stop=(c == CK - 1))
                        last.then_inc(sc_filled, 1)
                if f.exists():
                    n, i = f.n(), f.pair()
                    if f.second():
                        pe.wait_ge(final_done, (n - 1) * NB)
                    for b in range(NB):
                        if not f.second():
                            pe.wait_ge(z_done, f.eight() * NB + (b + 1))
                        ft = bank(pe, f, U_XT + b)
                        for c in range(CK):
                            last = pe.transpose(ft[:, c * 128:(c + 1) * 128], X[i][:, b, c * 128:(c + 1) * 128], identf[:, :])
                        last.then_inc(xT_filled, 1)
                if u.exists():
                    value_out(0)
                if f.exists():
                    ft = bank(pe, f, U_LT)
                    pe.wait_ge(xT_done, n * NB + NB)
                    for c in range(CK):
                        for half in range(2):
                            last = pe.matmul(ft[half * 32:half * 32 + 32, :], cw[:, c, :], XT[i][:, c, half * 4:half * 4 + 4].rearrange("p b t -> p (b t)"),
                                             start=(c == 0), stop=(c == CK - 1))
                    last.then_inc(lt_filled, 1)
                if u.exists():
                    for half in range(2):
                        pe.wait_ge(att_done, u.n() * 2 + (half + 1))
                        pe.wait_ge(sc_done, u.n() * 2 + (half + 1))
                        for b in range(4):
                            last = pe.transpose(SC[half][:, b * 128:(b + 1) * 128], att[:, half, b * 128:(b + 1) * 128], identf[:, :])
                        last.then_inc(attT_filled, 1)
                if f.exists():
                    ft = bank(pe, f, U_L)
                    pe.wait_ge(lt_done, n + 1)
                    for b in range(4):
                        last = pe.transpose(ft[:, b * 128:(b + 1) * 128], lt[:, b * 128:(b + 1) * 128], identf[:, :])
                    last.then_inc(l_filled, 1)
                if u.exists():
                    value_out(1)
                    mix(0)
                if f.exists():
                    ft = bank(pe, f, U_LG)
                    pe.wait_ge(lr_done, n + 1)
                    pe.transpose(ft[:, 0:128], lr[:, :, :].rearrange("p b s -> p (b s)"), identf[:, :]).then_inc(lg_filled, 1)
                if u.exists():
                    value_out(2)
                    mix(1)
                if f.exists():
                    ft = bank(pe, f, U_WT)
                    pe.wait_ge(w_top_done, n * 2 + 2)
                    pe.transpose(ft[:, 0:128], w_top[:, :], identf[:, :]).then_inc(wT_filled, 1)
                if u.exists():
                    value_out(3)
                    mix(2)
                if f.exists():
                    pe.wait_ge(wT_done, n + 1)
                    for half in range(2):
                        ft = bank(pe, f, U_G + half)
                        for b in range(4):
                            last = pe.matmul(ft[b * 32:(b + 1) * 32, :], WT[:, half * 4 + b, :], X[i][:, half * 4 + b, :], start=True, stop=True)
                        last.then_inc(g_filled, 1)
                if u.exists():
                    value_out(4)
                    mix(3)
                if f.exists():
                    for half in range(2):
                        ft = bank(pe, f, U_GT + half)
                        pe.wait_ge(g_done, n * 2 + (half + 1))
                        for c in range(CK):
                            last = pe.transpose(ft[:, c * 128:(c + 1) * 128], g[:, half, c * 128:(c + 1) * 128], identf[:, :])
                        last.then_inc(gT_filled, 1)
                if u.exists():
                    value_out(5)
                    mix(4)
                if f.exists():
                    if isinstance(n, int) and n == 0:
                        pe.wait_ge(big_in, 16 * 5)
                    ft = bank(pe, f, U_WR)
                    pe.wait_ge(gT_done, n * 2 + 2)
                    for c in range(CK):
                        last = pe.matmul(ft[:, :], gT[:, c].rearrange("p b s -> p (b s)"), write_sb[:, c, :], start=(c == 0), stop=(c == CK - 1))
                    last.then_inc(wr_filled, 1)
                if u.exists():
                    value_out(6)
                    mix(5)
                    value_out(7)
                if f.exists():
                    ft = bank(pe, f, U_WST)
                    pe.wait_ge(ws_done, n + 1)
                    for c in range(CK):
                        last = pe.transpose(ft[:, c * 128:(c + 1) * 128], ws[i][:, c * 128:(c + 1) * 128], identf[:, :])
                    last.then_inc(wsT_filled, 1)
                if u.exists():
                    mix(6)
                if f.exists():
                    pe.wait_ge(wsT_done, n + 1)
                    for use, w_sb in ((U_K, wk_sb), (U_V, wv_sb)):
                        ft = bank(pe, f, use)
                        for p in range(CK):
                            for c in range(CK):
                                last = pe.matmul(ft[:, p * 128:(p + 1) * 128], w_sb[:, c, p * 128:(p + 1) * 128], wsT[:, c, :],
                                                 start=(c == 0), stop=(c == CK - 1))
                        last.then_inc(kv_filled, 1)
                if u.exists():
                    mix(7)
                if f.exists():
                    pe.wait_ge(kd_done, n * 2 + 2)
                    for q in range(2):
                        ft = bank(pe, f, U_BIAS + q)
                        for p in range(2):
                            last = pe.matmul(ft[:, p * 256:(p + 1) * 256], bq_wide[:, 2 * q + p, :], kd[:, 2 * q + p].rearrange("p b h s -> p (b h s)"),
                                             start=True, stop=True)
                        last.then_inc(bias_filled, 1)
                    for c in range(CK):
                        for q in range(2):
                            ft = bank(pe, f, U_A + 2 * c + q)
                            for p in range(2):
                                last = pe.matmul(ft[:, p * 256:(p + 1) * 256], wq_sb[:, 2 * q + p, c * 128:(c + 1) * 128],
                                                 kd[:, 2 * q + p].rearrange("p b h s -> p (b h s)"), start=True, stop=True)
                            last.then_inc(a_filled, 1)
            units(pe, step)

        @block.scalar
        def _(act):
            act.wait_ge(small_in, 16 * (7 + 2 * NB))

            def step(f, u):
                def values(b):
                    m = u.n() * NB + b
                    act.wait_ge(vo_filled, m + 1)
                    at_least(act, xb_filled, m - 1)
                    act.activation(VO[b % 2][:, :], vo_ps[:, :], ACT.Copy).then_inc(vo_done, 1)

                def squares(b):
                    m = u.n() * NB + b
                    act.wait_ge(y_done, m + 1)
                    at_least(act, y_sq_done, m)
                    at_least(act, y_ms_done, m - 1)
                    act.activation(junk[:, :], y[:, b % 2, :], ACT.Square, accum_out=y_sq[:, b % 2:b % 2 + 1]).then_inc(y_sq_done, 1)

                if f.exists():
                    n, i = f.n(), f.pair()
                    for b in range(NB):
                        act.wait_ge(xT_filled, n * NB + (b + 1))
                        if b == 0:
                            at_least(act, sc_filled, (n - 1) * 2)
                        act.activation(XT[i][:, :, b, :], F[(U_XT + b) % 3][:, :].rearrange("p (c t) -> p c t", c=CK), ACT.Copy).then_inc(xT_done, 1)
                        if b % 4 == 3 and u.exists():
                            half = b // 4
                            act.wait_ge(sc_sub_done, u.n() * 2 + (half + 1))
                            at_least(act, att_done, (u.n() - 1) * 2 + (half + 1))
                            act.activation(sc_exp[:, half, :], sc[:, half, :], ACT.Exp, scale=SCALE).then_inc(sc_exp_done, 1)
                elif u.exists():
                    for half in range(2):
                        act.wait_ge(sc_sub_done, u.n() * 2 + (half + 1))
                        at_least(act, att_done, (u.n() - 1) * 2 + (half + 1))
                        act.activation(sc_exp[:, half, :], sc[:, half, :], ACT.Exp, scale=SCALE).then_inc(sc_exp_done, 1)
                if u.exists():
                    values(0)
                if f.exists():
                    act.wait_ge(lt_filled, n + 1)
                    at_least(act, l_filled, n)
                    act.activation(lt[0:64, :], F[U_LT % 3][0:64, :], ACT.Copy).then_inc(lt_done, 1)
                    for b in range(NB):
                        at_least(act, x_ms_done, n) if b == 0 else None
                        act.wait_ge(x_sq_done, n * NB + b) if not (isinstance(n, int) and n * NB + b == 0) else None
                        act.activation(junk2[:, :], X[i][:, b, :], ACT.Square, accum_out=x_sq[:, b:b + 1]).then_inc(x_sq_done, 1)
                if u.exists():
                    for half in range(2):
                        act.wait_ge(attT_filled, u.n() * 2 + (half + 1))
                        at_least(act, xb_filled, (u.n() - 1) * NB + (half * 4 + 4))
                        act.activation(attT[half][:, :, :], SC[half][:, :].rearrange("p (b t) -> p b t", b=4), ACT.Copy).then_inc(attT_done, 1)
                    values(1)
                    squares(0)
                    values(2)
                if f.exists():
                    act.wait_ge(top_chain, n * 6 + 2)
                    at_least(act, top_chain, (n - 1) * 6 + 6)
                    act.activation(e_top[:, :], lg[:, 0:128], ACT.Exp, bias=neg_top[:, :]).then_inc(e_top_done, 1)
                if u.exists():
                    squares(1)
                    values(3)
                    squares(2)
                if f.exists():
                    for half in range(2):
                        act.wait_ge(g_filled, n * 2 + (half + 1))
                        at_least(act, gT_filled, (n - 1) * 2 + (half + 1))
                        act.activation(g[:, half, :], F[(U_G + half) % 3][:, :], ACT.Copy).then_inc(g_done, 1)
                if u.exists():
                    values(4)
                    squares(3)
                    values(5)
                    squares(4)
                if f.exists():
                    act.wait_ge(ws_sum_done, n + 1)
                    at_least(act, ws_ms_done, n)
                    at_least(act, ws_sq_done, n)
                    act.activation(junk2[:, :], ws_sum[:, :], ACT.Square, accum_out=ws_sq[:, :]).then_inc(ws_sq_done, 1)
                if u.exists():
                    values(6)
                    squares(5)
                    values(7)
                if f.exists():
                    act.wait_ge(wsT_filled, n + 1)
                    at_least(act, kv_filled, n * 2)
                    act.activation(wsT[:, :, :], F[U_WST % 3][:, :].rearrange("p (c r) -> p c r", c=CK), ACT.Copy).then_inc(wsT_done, 1)
                if u.exists():
                    squares(6)
                    squares(7)
                if f.exists():
                    for q in range(2):
                        act.wait_ge(bias_filled, n * 2 + (q + 1))
                        if q == 0:
                            at_least(act, sc_done, n * 2)
                        act.activation(s_bias[:, :, 2 * q:2 * q + 2, :].rearrange("p b c s -> p c b s"),
                                       F[(U_BIAS + q) % 3][:, :].rearrange("p (c b s) -> p c b s", c=2, b=NB), ACT.Copy).then_inc(bias_done, 1)
                    for c in range(CK):
                        for q in range(2):
                            act.wait_ge(a_filled, n * 2 * CK + (2 * c + q + 1))
                            if c == 0 and q == 0:
                                at_least(act, sc_filled, n * 2)
                            act.activation(A[:, c, :, 2 * q:2 * q + 2, :].rearrange("p b c s -> p c b s"),
                                           F[(U_A + 2 * c + q) % 3][:, :].rearrange("p (c b s) -> p c b s", c=2, b=NB), ACT.Copy).then_inc(a_done, 1)
            units(act, step)


def decoder(nc, x, ctx, ctxT, ident, hadamard, after, causal_cols, w_upT, w_downT, workspace, compete_wT, compete_b,
            write_wT, write_b, wq, wkT, wvT, in_proj_cols, out_wT, out_b, pre_cols, norm_post, out):
    B, T, C = x.shape

    def scratch(name, shape, dt=F32):
        return nc.dram_tensor(name, shape, dt).ap()

    q_parts, k_parts = scratch("q_parts", (B, 3, T, C), BF16), scratch("k_parts", (B, 3, T, C), BF16)
    heads_out, recips = scratch("heads_out", (2 * B, 128, C)), scratch("recips", (B, 128, 32))
    x2, x3 = scratch("x2", (B, T, C)), scratch("x3", (B, T, C))
    attention0(nc, x, ctx, ctxT, ident, q_parts, k_parts, heads_out)
    ternary_ffn(nc, x, heads_out, recips, hadamard, ident, w_upT, w_downT, x2)
    causal_attention(nc, x2, ctx, ctxT, ident, after, causal_cols, x3)
    workspace_ffn(nc, x3, ident, workspace, compete_wT, compete_b, write_wT, write_b, wq, wkT, wvT, in_proj_cols,
                  out_wT, out_b, pre_cols, norm_post, out)


def kernel(**inputs):
    import numpy as _np
    import concourse.bacc as _bacc
    from concourse import mybir as _mybir
    from concourse.bass_utils import run_bass_kernel_spmd as _run

    a = {name: _np.asarray(value) for name, value in inputs.items()}
    x, ctx = a["x"], a["ctx_2048"]
    B, T, C = x.shape
    in_w = a["L1_ffn_in_proj_w"]
    F = _np.float32

    hadamard = _np.ones((1, 1), F)
    while hadamard.shape[0] < 128:
        hadamard = _np.block([[hadamard, hadamard], [hadamard, -hadamard]])
    token = _np.arange(T)
    masked_score, head_channels = -10000.0, C // 16
    causal_cols = _np.stack([_np.full(T, -masked_score * float(head_channels) ** 0.5), _np.full(T, masked_score), T - 1.0 - token], 1).astype(F)
    causal_cols[T - 1, :2] = 3e38, -3e38

    laid_out = {
        "x": x, "ctx": ctx, "ctxT": ctx.transpose(0, 2, 1), "ident": _np.eye(128, dtype=F), "hadamard": hadamard,
        "after": (token[:, None] > token[None, :]).astype(F), "causal_cols": causal_cols,
        "w_upT": a["L0_ffn_w_up"].T, "w_downT": a["L0_ffn_w_down"].T,
        "workspace": a["L1_ffn_workspace"], "compete_wT": a["L1_ffn_compete_w"].T, "compete_b": a["L1_ffn_compete_b"],
        "write_wT": a["L1_ffn_write_w"].T, "write_b": a["L1_ffn_write_b"],
        "wq": in_w[:C], "wkT": in_w[C:2 * C].T, "wvT": in_w[2 * C:].T,
        "in_proj_cols": a["L1_ffn_in_proj_b"].reshape(3, C // 128, 128).transpose(2, 0, 1),
        "out_wT": a["L1_ffn_out_proj_w"].T, "out_b": a["L1_ffn_out_proj_b"],
        "pre_cols": a["L1_ffn_norm_pre_w"].reshape(C // 128, 128).T, "norm_post": a["L1_ffn_norm_post_w"],
    }
    nc = _bacc.Bacc("TRN2", target_bir_lowering=False, num_devices=1)
    arrays, args = {}, {}
    for name, array in laid_out.items():
        array = _np.ascontiguousarray(array)
        arrays[f"in_{name}_dram"] = array
        args[name] = nc.dram_tensor(f"in_{name}_dram", array.shape, _mybir.dt.from_np(array.dtype), kind="ExternalInput").ap()
    args["out"] = nc.dram_tensor("out_dram", (B, T, C), _mybir.dt.float32, kind="ExternalOutput").ap()
    decoder(nc, **args)
    return _run(nc, [arrays], core_ids=[0]).results[0]["out_dram"]
```
